# Optimizing a Trainium2 kernel written in Bass

```python
import numpy as np
import jax
import jax.numpy as jnp

def _softmax(x, axis=-1):
    return jax.nn.softmax(x, axis=axis)

def _gelu(x):
    return jax.nn.gelu(x, approximate=True)

def _silu(x):
    return jax.nn.silu(x)

def _sigmoid(x):
    return jax.nn.sigmoid(x)

def _layernorm(x, axis=-1, eps=1e-05):
    m = jnp.mean(x, axis=axis, keepdims=True)
    v = jnp.var(x, axis=axis, keepdims=True)
    return (x - m) / jnp.sqrt(v + eps)

def _scatter_add(tgt, idx, src, axis=0):
    return tgt.at[idx].add(src)

def _segment_sum(src, seg, n):
    return jax.ops.segment_sum(src, seg, n)
kernel_name = 'mk_adj_ffn_d2_adj_r2_f5fae4'

def setup_inputs(seed: int=0):
    np.random.seed(seed)
    _w = jnp.asarray

    def _rec_inputs():
        import jax
        import jax.numpy as jnp
        _gk = jax.random.key(seed)
        x = -0.0002928 + 1 * jax.random.normal(jax.random.fold_in(_gk, 1), (1354, 256), jnp.float32)
        _w = (1.0 + jnp.arange(1354, dtype=jnp.float32)) ** (-0.5)
        _w = _w / _w.mean()
        _pij = jnp.clip(0.0014771 * _w[:, None] * _w[None, :], 0.0, 1.0)
        _a = jax.random.uniform(jax.random.fold_in(_gk, 2), (1354, 1354)) < _pij
        _a = jnp.logical_or(_a, jnp.eye(1354, dtype=bool))
        _af = _a.astype(jnp.float32)
        _af = _af * jax.random.uniform(jax.random.fold_in(_gk, 3), (1354, 1354), jnp.float32, 0.05, 1)
        adj = _af
        return (x, adj)
    x, adj = _rec_inputs()

    def _L0_gnn_setup():
        import jax, jax.numpy as jnp
        import numpy as np
        N = 4096
        D = 256
        key = jax.random.key(seed)
        k1, k2 = jax.random.split(key)
        inp = jax.random.normal(k1, (N, D), dtype=jnp.float32)
        A = jax.random.uniform(k2, (N, N), dtype=jnp.float32)
        W = jnp.ones((D,), dtype=jnp.float32)
        return {'input': inp, 'A': A, 'W': W}
    _L0_gnn_all = _L0_gnn_setup()
    _L0_gnn_in = {k: v for k, v in _L0_gnn_all.items() if k in ('W',)}
    del _L0_gnn_all

    def _L0_ffn_setup():
        import jax, jax.numpy as jnp
        import numpy as np
        D_MODEL = 256
        D_FF = 1024
        N_HEADS = 8
        N_EXPERTS = 8
        TOP_K = 2
        CAPACITY_FACTOR = 1.6
        BATCH = 2048
        SEQ = 16
        LN_EPS = 1e-05

        def _layernorm(x, g, b):
            mu = x.mean(-1, keepdims=True)
            var = ((x - mu) ** 2).mean(-1, keepdims=True)
            return (x - mu) * jax.lax.rsqrt(var + LN_EPS) * g + b

        def _moe(xf, router_w, router_b, w1, b1, w2, b2):
            T = xf.shape[0]
            probs = jax.nn.softmax(xf @ router_w + router_b, axis=-1)
            _, topk_idx = jax.lax.top_k(probs, TOP_K)
            capacity = int(np.ceil(T * CAPACITY_FACTOR / N_EXPERTS))
            out = jnp.zeros_like(xf)
            tok = jnp.arange(T)
            for i in range(N_EXPERTS):
                mask = (topk_idx == i).any(-1)
                pos = jnp.where(mask, tok, T)
                sel = jnp.sort(pos)[:capacity]
                xi = xf[jnp.minimum(sel, T - 1)]
                hi = jax.nn.gelu(xi @ w1[i] + b1[i], approximate=False)
                yi = hi @ w2[i] + b2[i]
                out = out.at[sel].set(yi, mode='drop')
            return out
        key = jax.random.key(seed)
        ks = jax.random.split(key, 24)
        s = 0.02
        d, f, e = (D_MODEL, D_FF, N_EXPERTS)
        inp = {'x': jax.random.normal(ks[0], (BATCH, SEQ, d), dtype=jnp.float32), 'ln1_g': jnp.ones((d,), jnp.float32), 'ln1_b': jnp.zeros((d,), jnp.float32), 'ln2_g': jnp.ones((d,), jnp.float32), 'ln2_b': jnp.zeros((d,), jnp.float32), 'wq': jax.random.normal(ks[1], (d, d)) * s, 'bq': jnp.zeros((d,)), 'wk': jax.random.normal(ks[2], (d, d)) * s, 'bk': jnp.zeros((d,)), 'wv': jax.random.normal(ks[3], (d, d)) * s, 'bv': jnp.zeros((d,)), 'wo': jax.random.normal(ks[4], (d, d)) * s, 'bo': jnp.zeros((d,)), 'router_w': jax.random.normal(ks[5], (d, e)) * s, 'router_b': jnp.zeros((e,)), 'w1': jax.random.normal(ks[6], (e, d, f)) * s, 'b1': jnp.zeros((e, f)), 'w2': jax.random.normal(ks[7], (e, f, d)) * s, 'b2': jnp.zeros((e, d))}
        return inp
    _L0_ffn_all = _L0_ffn_setup()
    _L0_ffn_in = {k: v for k, v in _L0_ffn_all.items() if k in ('ln1_g', 'ln1_b', 'ln2_g', 'ln2_b', 'wq', 'bq', 'wk', 'bk', 'wv', 'bv', 'wo', 'bo', 'router_w', 'router_b', 'w1', 'b1', 'w2', 'b2')}
    del _L0_ffn_all

    def _L1_gnn_setup():
        import jax, jax.numpy as jnp
        import numpy as np
        N, IN_DIM, OUT_DIM = (4096, 256, 256)
        ALPHA = 0.2
        EPS = 1e-09
        key = jax.random.key(seed)
        k1, k2, k3, k4, k5 = jax.random.split(key, 5)
        feat = jax.random.normal(k1, (N, IN_DIM), dtype=jnp.float32)
        counting_attn = jax.random.uniform(k2, (N, N), dtype=jnp.float32)
        W = jax.random.normal(k3, (IN_DIM, OUT_DIM), dtype=jnp.float32) / np.sqrt(IN_DIM)
        attn_l = jax.random.normal(k4, (OUT_DIM, 1), dtype=jnp.float32) * 0.1
        attn_r = jax.random.normal(k5, (OUT_DIM, 1), dtype=jnp.float32) * 0.1
        return {'feat': feat, 'counting_attn': counting_attn, 'W': W, 'attn_l': attn_l, 'attn_r': attn_r}
    _L1_gnn_all = _L1_gnn_setup()
    _L1_gnn_in = {k: v for k, v in _L1_gnn_all.items() if k in ('W', 'attn_l', 'attn_r')}
    del _L1_gnn_all

    def _L1_ffn_setup():
        import jax, jax.numpy as jnp
        import numpy as np
        NUM_EXPERTS = 8
        TOP_K = 2
        HIDDEN = 256
        INTERMEDIATE = 1024
        BATCH, SEQ = (8, 1024)
        key = jax.random.key(seed)
        ks = jax.random.split(key, 7)
        s_in = 1.0 / np.sqrt(HIDDEN)
        s_mid = 1.0 / np.sqrt(INTERMEDIATE)
        return {'x': jax.random.normal(ks[0], (BATCH, SEQ, HIDDEN), jnp.float32), 'Wg': jax.random.normal(ks[1], (HIDDEN, NUM_EXPERTS), jnp.float32) * s_in, 'bg': jnp.zeros((NUM_EXPERTS,), jnp.float32), 'W1': jax.random.normal(ks[2], (NUM_EXPERTS, HIDDEN, INTERMEDIATE), jnp.float32) * s_in, 'b1': jnp.zeros((NUM_EXPERTS, INTERMEDIATE), jnp.float32), 'W2': jax.random.normal(ks[3], (NUM_EXPERTS, INTERMEDIATE, HIDDEN), jnp.float32) * s_mid, 'b2': jnp.zeros((NUM_EXPERTS, HIDDEN), jnp.float32)}
    _L1_ffn_all = _L1_ffn_setup()
    _L1_ffn_in = {k: v for k, v in _L1_ffn_all.items() if k in ('Wg', 'bg', 'W1', 'b1', 'W2', 'b2')}
    del _L1_ffn_all
    return {'x': x, 'adj': adj, 'L0_gnn_W': _L0_gnn_in['W'], 'L0_ffn_ln1_g': _L0_ffn_in['ln1_g'], 'L0_ffn_ln1_b': _L0_ffn_in['ln1_b'], 'L0_ffn_ln2_g': _L0_ffn_in['ln2_g'], 'L0_ffn_ln2_b': _L0_ffn_in['ln2_b'], 'L0_ffn_wq': _L0_ffn_in['wq'], 'L0_ffn_bq': _L0_ffn_in['bq'], 'L0_ffn_wk': _L0_ffn_in['wk'], 'L0_ffn_bk': _L0_ffn_in['bk'], 'L0_ffn_wv': _L0_ffn_in['wv'], 'L0_ffn_bv': _L0_ffn_in['bv'], 'L0_ffn_wo': _L0_ffn_in['wo'], 'L0_ffn_bo': _L0_ffn_in['bo'], 'L0_ffn_router_w': _L0_ffn_in['router_w'], 'L0_ffn_router_b': _L0_ffn_in['router_b'], 'L0_ffn_w1': _L0_ffn_in['w1'], 'L0_ffn_b1': _L0_ffn_in['b1'], 'L0_ffn_w2': _L0_ffn_in['w2'], 'L0_ffn_b2': _L0_ffn_in['b2'], 'L1_gnn_W': _L1_gnn_in['W'], 'L1_gnn_attn_l': _L1_gnn_in['attn_l'], 'L1_gnn_attn_r': _L1_gnn_in['attn_r'], 'L1_ffn_Wg': _L1_ffn_in['Wg'], 'L1_ffn_bg': _L1_ffn_in['bg'], 'L1_ffn_W1': _L1_ffn_in['W1'], 'L1_ffn_b1': _L1_ffn_in['b1'], 'L1_ffn_W2': _L1_ffn_in['W2'], 'L1_ffn_b2': _L1_ffn_in['b2']}

def reference(x, adj, L0_gnn_W, L0_ffn_ln1_g, L0_ffn_ln1_b, L0_ffn_ln2_g, L0_ffn_ln2_b, L0_ffn_wq, L0_ffn_bq, L0_ffn_wk, L0_ffn_bk, L0_ffn_wv, L0_ffn_bv, L0_ffn_wo, L0_ffn_bo, L0_ffn_router_w, L0_ffn_router_b, L0_ffn_w1, L0_ffn_b1, L0_ffn_w2, L0_ffn_b2, L1_gnn_W, L1_gnn_attn_l, L1_gnn_attn_r, L1_ffn_Wg, L1_ffn_bg, L1_ffn_W1, L1_ffn_b1, L1_ffn_W2, L1_ffn_b2):
    import jax
    import jax.numpy as jnp

    def _L0_gnn_ref(input, A, W):
        import jax, jax.numpy as jnp
        import numpy as np
        N = 4096
        D = 256
        hidden = input * W
        return A @ hidden

    def _L0_ffn_ref(x, ln1_g, ln1_b, ln2_g, ln2_b, wq, bq, wk, bk, wv, bv, wo, bo, router_w, router_b, w1, b1, w2, b2):
        import jax, jax.numpy as jnp
        import numpy as np
        D_MODEL = 256
        D_FF = 1024
        N_HEADS = 8
        N_EXPERTS = 8
        TOP_K = 2
        CAPACITY_FACTOR = 1.6
        BATCH = 2048
        SEQ = 16
        LN_EPS = 1e-05

        def _layernorm(x, g, b):
            mu = x.mean(-1, keepdims=True)
            var = ((x - mu) ** 2).mean(-1, keepdims=True)
            return (x - mu) * jax.lax.rsqrt(var + LN_EPS) * g + b

        def _moe(xf, router_w, router_b, w1, b1, w2, b2):
            T = xf.shape[0]
            probs = jax.nn.softmax(xf @ router_w + router_b, axis=-1)
            _, topk_idx = jax.lax.top_k(probs, TOP_K)
            capacity = int(np.ceil(T * CAPACITY_FACTOR / N_EXPERTS))
            out = jnp.zeros_like(xf)
            tok = jnp.arange(T)
            for i in range(N_EXPERTS):
                mask = (topk_idx == i).any(-1)
                pos = jnp.where(mask, tok, T)
                sel = jnp.sort(pos)[:capacity]
                xi = xf[jnp.minimum(sel, T - 1)]
                hi = jax.nn.gelu(xi @ w1[i] + b1[i], approximate=False)
                yi = hi @ w2[i] + b2[i]
                out = out.at[sel].set(yi, mode='drop')
            return out
        B, S, D = x.shape
        dk = D // N_HEADS
        h = _layernorm(x, ln1_g, ln1_b)
        q = (h @ wq + bq).reshape(B, S, N_HEADS, dk)
        k = (h @ wk + bk).reshape(B, S, N_HEADS, dk)
        v = (h @ wv + bv).reshape(B, S, N_HEADS, dk)
        scores = jnp.einsum('bqhd,bkhd->bhqk', q, k) / np.sqrt(dk).astype(np.float32)
        attn = jax.nn.softmax(scores, axis=-1)
        ctx = jnp.einsum('bhqk,bkhd->bqhd', attn, v).reshape(B, S, D)
        x = x + ctx @ wo + bo
        h2 = _layernorm(x, ln2_g, ln2_b)
        moe_out = _moe(h2.reshape(-1, D), router_w, router_b, w1, b1, w2, b2)
        return x + moe_out.reshape(B, S, D)

    def _L1_gnn_ref(feat, counting_attn, W, attn_l, attn_r):
        import jax, jax.numpy as jnp
        import numpy as np
        N, IN_DIM, OUT_DIM = (4096, 256, 256)
        ALPHA = 0.2
        EPS = 1e-09
        h = feat @ W
        a1 = h @ attn_l
        a2 = h @ attn_r
        a = jax.nn.leaky_relu(a1 + a2.T, ALPHA)
        a = a - jnp.max(a, axis=1, keepdims=True)
        nomi = jnp.exp(a) * counting_attn
        deno = jnp.sum(nomi, axis=1, keepdims=True)
        a_nor = nomi / (deno + EPS)
        ret = jax.nn.elu(a_nor @ h)
        return ret

    def _L1_ffn_ref(x, Wg, bg, W1, b1, W2, b2):
        import jax, jax.numpy as jnp
        import numpy as np
        NUM_EXPERTS = 8
        TOP_K = 2
        HIDDEN = 256
        INTERMEDIATE = 1024
        BATCH, SEQ = (8, 1024)
        B, S, H = x.shape
        xf = x.reshape(B * S, H)
        logits = xf @ Wg + bg
        probs = jax.nn.softmax(logits, axis=-1)
        _, top_idx = jax.lax.top_k(probs, TOP_K)
        mask = jnp.any(top_idx[:, :, None] == jnp.arange(NUM_EXPERTS)[None, None, :], axis=1)
        comb = probs * mask.astype(probs.dtype)
        out = jnp.zeros_like(xf)
        for e in range(NUM_EXPERTS):
            h = jax.nn.gelu(xf @ W1[e] + b1[e])
            y = h @ W2[e] + b2[e]
            out = out + comb[:, e:e + 1] * y
        return out.reshape(B, S, H)
    x = x + _L0_gnn_ref(_layernorm(x, axis=-1), adj, L0_gnn_W)
    x = x + _L0_ffn_ref(_layernorm(x, axis=-1)[None], L0_ffn_ln1_g, L0_ffn_ln1_b, L0_ffn_ln2_g, L0_ffn_ln2_b, L0_ffn_wq, L0_ffn_bq, L0_ffn_wk, L0_ffn_bk, L0_ffn_wv, L0_ffn_bv, L0_ffn_wo, L0_ffn_bo, L0_ffn_router_w, L0_ffn_router_b, L0_ffn_w1, L0_ffn_b1, L0_ffn_w2, L0_ffn_b2)[0]
    x = x + _L1_gnn_ref(_layernorm(x, axis=-1), adj, L1_gnn_W, L1_gnn_attn_l, L1_gnn_attn_r)
    x = x + _L1_ffn_ref(_layernorm(x, axis=-1)[None], L1_ffn_Wg, L1_ffn_bg, L1_ffn_W1, L1_ffn_b1, L1_ffn_W2, L1_ffn_b2)[0]
    return x

_drawn_inputs = setup_inputs


def setup_inputs(seed=0):
    import zlib

    import numpy as np

    out = dict(_drawn_inputs(seed))
    spreads = {'L0_gnn_W': (1.0, 0.2),
     'L0_ffn_ln1_g': (1.0, 0.6),
     'L0_ffn_ln1_b': (0.0, 0.77),
     'L0_ffn_ln2_g': (1.0, 0.2),
     'L0_ffn_ln2_b': (0.0, 0.287),
     'L0_ffn_bq': (0.0, 0.8),
     'L0_ffn_bk': (0.0, 2.0),
     'L0_ffn_bv': (0.0, 0.436),
     'L0_ffn_bo': (0.0, 0.283),
     'L0_ffn_router_b': (0.0, 0.1),
     'L0_ffn_b1': (0.0, 0.584),
     'L0_ffn_b2': (0.0, 0.366),
     'L1_ffn_bg': (0.0, 0.363),
     'L1_ffn_b1': (0.0, 0.748),
     'L1_ffn_b2': (0.0, 0.509)}
    factors = {'L0_ffn_wq': 8.0,
     'L0_ffn_wk': 8.0,
     'L0_ffn_wv': 7.384,
     'L0_ffn_wo': 2.88,
     'L1_gnn_attn_l': 3.589}
    for name, (base, spread) in spreads.items():
        noise = np.random.default_rng([zlib.crc32(name.encode()), seed]).standard_normal(out[name].shape)
        drawn = base * np.exp(spread * noise) if base else spread * noise
        out[name] = jnp.asarray(drawn.astype(out[name].dtype))
    for name, factor in factors.items():
        out[name] = (out[name] * factor).astype(out[name].dtype)
    return out
```

```python
from contextlib import ExitStack

import numpy as np

import concourse.bass as bass
from concourse import mybir

F32 = mybir.dt.float32
F32R = mybir.dt.float32r
BF16 = mybir.dt.bfloat16
I32 = mybir.dt.int32
ALU = mybir.AluOpType
ACT = mybir.ActivationFunctionType
AX_X = mybir.AxisListType.X

P = 128
N = 1354
D = 256
DT = D // P
T = -(-N // P)
NP = T * P
LAST = N - (T - 1) * P
H = 8
DK = D // H
QC = 340
QB = 4
HALF = 2 * QC
NC4 = NP // QB
E = 8
F = 1024
FT = F // P
CAP = int(np.ceil(N * 1.6 / E))
CAPP = CAP + CAP % 2
CT = -(-CAPP // P)
CREM = CAPP - (CT - 1) * P
SLOTS0 = E * CAPP
TILES1 = (2 * N + E * (P - 1)) // P
SLOTS1 = TILES1 * P
WCOLS = DT * F + FT * D + FT + DT
B1AT = DT * F + FT * D
B2AT = B1AT + FT
W1COLS = B2AT
FAR = 1.0e6
UNDER = -87.3365
EPS = 1e-5
SCALE = float(1.0 / np.sqrt(np.float32(DK)))
GA = 8
GB = T - GA

C_ID = 0
C_TRI = C_ID + P
C_VALID = C_TRI + P
C_LT = C_VALID + T
C_OFF = C_LT + E * E
C_LE = C_OFF + E
C_K = C_LE + E * E
C_TILE = C_K + T
C_END = C_TILE + TILES1 + 1

V_G1, V_B1, V_G2, V_B2, V_BQ, V_BK = (2 * i for i in range(6))
V_RB, V_GB = 12, 13
V_END = 14


def shape_constants():
    c = np.zeros((P, C_END), np.float32)
    c[:, C_ID:C_ID + P] = np.eye(P)
    c[:, C_TRI:C_TRI + P] = np.triu(np.ones((P, P)), 1)
    tok = np.arange(T)[None, :] * P + np.arange(P)[:, None]
    c[:, C_VALID:C_VALID + T] = tok < N
    j, i = np.meshgrid(np.arange(E), np.arange(E), indexing="ij")
    c[:, C_LT:C_LT + E * E] = (j < i).reshape(1, -1)
    c[:, C_OFF:C_OFF + E] = np.arange(E) * CAPP + 1
    c[:, C_LE:C_LE + E * E] = (i <= j).reshape(1, -1)
    c[:, C_K:C_K + T] = np.arange(T) * P
    c[:, C_TILE:C_TILE + TILES1 + 1] = np.arange(TILES1 + 1)
    return c


def build_program(nc, a, out):
    with ExitStack() as ctx:
        base = -(-nc.sbuf_base // 32) * 32
        top = nc.sbuf_top
        cursor = [base]

        offsets = {}

        def place(name, shape, dtype=F32, parts=P):
            offsets[name] = cursor[0]
            size = int(np.prod(shape)) * (2 if dtype == BF16 else 4)
            t = nc.alloc_sbuf_tensor_at(name, [parts] + list(shape), dtype, offset=cursor[0])
            cursor[0] += -(-size // 32) * 32
            assert cursor[0] <= top, (name, cursor[0], top)
            return t

        x_res = place("x_res", [T, D])
        u_or_h = place("u_or_h", [T * (D + 2)])
        u = u_or_h[:, 0:T * D].rearrange("p (t d) -> p t d", t=T)
        hg = u_or_h[:, :].rearrange("p (t d) -> p t d", t=T)
        nat = place("nat", [T, D])
        nt = place("nt", [DT, NP])
        const = place("const", [C_END])
        ones = place("ones", [P])
        tri_b = place("tri_b", [P], BF16)
        ones_b = place("ones_b", [P], BF16)
        vecs = place("vecs", [V_END])
        rows = place("rows", [3, D])
        w_attn = place("w_attn", [4, DT, D])
        w_graph = place("w_graph", [DT, D + 2])
        w_graph_t = place("w_graph_t", [DT, D])
        attn_lr = place("attn_lr", [DT, 2])
        w_router = place("w_router", [2, DT, E])
        b2_l1 = place("b2_l1", [D], F32, E)
        stats = place("stats", [T, 6])
        mv = place("mv", [T, 2])
        var = place("var", [T])
        std = place("std", [T])
        rstd = place("rstd", [T])
        lgt = place("lgt", [NP], F32, E)
        lg = place("lg", [T, E])
        top1 = place("top1", [T])
        probs = place("probs", [T, E])
        psum_e = place("psum_e", [T])
        cmp_gt = place("cmp_gt", [T, E, E])
        cmp_eq = place("cmp_eq", [T, E, E])
        mask = place("mask", [T, E])
        mask_b = place("mask_b", [T, E], BF16)
        slot = place("slot", [T, E])
        sa = place("sa", [T])
        sb_ = place("sb_", [T])
        skip = place("skip", [T])
        idx = place("idx", [2, T], I32)
        comb = place("comb", [T, E])
        ca = place("ca", [T])
        cb = place("cb", [T])
        cnt = place("cnt", [E])
        tiles_e = place("tiles_e", [E])
        ends = place("ends", [E])
        starts = place("starts", [E])
        texp = place("texp", [TILES1 + 1])
        tile_expert = place("tile_expert", [TILES1 + 1], I32)
        zeros = place("zeros", [D])
        arena = cursor[0]
        assert arena + E * W1COLS * 4 <= top, (arena, top)

        w_l1 = place("w_l1", [E, W1COLS])
        half_l1 = arena + 4 * W1COLS * 4
        cursor[0] = arena
        adj0 = [place(f"adj0_{i}", [NP]) for i in range(3)]
        cursor[0] = arena
        w_l0 = [place(f"w_l0_{i}", [WCOLS]) for i in range(2)]
        attn_at = cursor[0]
        v_nat = place("v_nat", [T, D])
        v_st = [place(f"v_st{i}", [T, 2 * DK]) for i in range(2)]
        q_st = [place(f"q_st{i}", [NP], F32R) for i in range(2)]
        k_st = [place(f"k_st{i}", [NP], F32R) for i in range(2)]
        expo = [place(f"expo{i}", [HALF]) for i in range(2)]
        proj = [place(f"proj{i}", [NC4]) for i in range(2)]
        proj_hi = [place(f"proj_hi{i}", [NC4], F32R) for i in range(2)]
        proj_lo = [place(f"proj_lo{i}", [NC4], F32R) for i in range(2)]
        ctx_raw = [place(f"ctx_raw{i}", [HALF], F32, 2 * DK) for i in range(2)]
        ctx_inv = place("ctx_inv", [HALF], F32, DK)
        ctx_n = [place(f"ctx_n{i}", [NP], F32, DK) for i in range(2)]
        mx4 = place("mx4", [T, QB])
        negm = place("negm", [T])
        m_hl = place("m_hl", [2 * T], F32R)
        m_rows = place("m_rows", [P], F32R, 2 * T)
        cursor[0] = attn_at
        xs0 = [place(f"xs0_{i}", [CT, D]) for i in range(2)]
        xs0_t = place("xs0_t", [DT, CAPP])
        h0 = place("h0", [FT, CAPP])
        y0_t = place("y0_t", [DT, CAPP])
        y0 = [place(f"y0_{i}", [CT, D]) for i in range(2)]
        assert cursor[0] <= half_l1
        cursor[0] = arena
        adj1 = [place(f"adj1_{i}", [NP]) for i in range(3)]
        wgt = [place(f"wgt{i}", [NP]) for i in range(3)]
        wgt_keep = place("wgt_keep", [T, GB * P])
        a12 = place("a12", [T, 2])
        a_max = place("a_max", [1])
        a_maxr = place("a_maxr", [P], F32, 1)
        a_max1 = place("a_max1", [1], F32, 1)
        a_all = place("a_all", [1])
        csum = place("csum", [T])
        cneg = place("cneg", [T])
        cpos = place("cpos", [T])
        agap = place("agap", [T])
        pq = place("pq", [2, T])
        fg = place("fg", [2, T])
        den = place("den", [T])
        assert cursor[0] <= half_l1
        ident = const[:, C_ID:C_ID + P]
        valid = const[:, C_VALID:C_VALID + T]
        diag = nat[:, :, :].rearrange("p t d -> p (t d)").rearrange("p (k c) -> p k c", c=P)
        pq_rows = nt
        z = nat
        cursor[0] = offsets["w_attn"]
        x1t = place("x1t", [D])
        x1t_t = place("x1t_t", [DT, P])
        y1t = place("y1t", [D])
        assert cursor[0] <= offsets["w_graph"]
        cursor[0] = offsets["nt"]
        h1pre = place("h1pre", [F])
        h1 = place("h1", [FT, P])
        assert cursor[0] <= offsets["const"]
        comb_t = lgt

        ps = ctx.enter_context(nc.psum_tensor("ps", [P, 8, 512], F32))

        def scratch(name, shape):
            return nc.dram_tensor(name, shape, F32, kind="Internal").ap()

        q_hi_d, q_lo_d, k_hi_d, k_lo_d = (scratch(n, [D, NP]) for n in ("q_hi_d", "q_lo_d", "k_hi_d", "k_lo_d"))
        ctx_d = scratch("ctx_d", [D, NP])
        xs0_d, ys0_d = scratch("xs0_d", [SLOTS0, D]), scratch("ys0_d", [SLOTS0, D])
        xs1_d, ys1_d = scratch("xs1_d", [SLOTS1, D]), scratch("ys1_d", [SLOTS1, D])

        def sem(name):
            return ctx.enter_context(nc.semaphore(name))

        s_x = sem("x_loaded")
        s_const = sem("const_loaded")
        s_wts = sem("small_weights_loaded")
        s_adj0 = [sem(f"adj0_loaded{i}") for i in range(3)]
        s_ones = sem("ones_ready")
        s_step = sem("dve_step")
        s_var = sem("variance_ready")
        s_std = sem("std_ready")
        s_nat = sem("normed_ready")
        s_hid = sem("hidden_ready")
        s_g0_row = sem("graph0_row_done")
        s_x1 = sem("x1_ready")
        s_tr = sem("transposes_done")
        s_tr_act = sem("transposed_by_act")
        s_tr_dve = sem("transposed_by_dve")
        s_qk_ps = sem("qk_product_done")
        s_qk_raw = sem("qk_biased")
        s_qk_hi = sem("qk_high_ready")
        s_qk_lo = sem("qk_low_ready")
        s_qk_out = [sem(f"qk_written{i}") for i in range(2)]
        s_v_ps = sem("v_product_done")
        s_vz = sem("v_pad_zeroed")
        s_v = sem("v_ready")
        s_v_st = sem("v_stack_ready")
        s_stack = [sem(f"qk_stack_loaded{i}") for i in range(2)]
        s_kone = sem("k_ones_ready")
        s_s1 = sem("scores_for_max_done")
        s_mx = sem("chunk_max_ready")
        s_mq = sem("max_stats_step")
        s_hl = sem("neg_max_ready")
        s_mt = sem("neg_max_transposed")
        s_mrow = sem("neg_max_rows_ready")
        s_mload = [sem(f"neg_max_loaded{i}") for i in range(2)]
        s_s2 = sem("scores_done")
        s_exp = sem("exp_ready")
        s_av = sem("attn_product_done")
        s_cr_act = sem("ctx_copied_by_act")
        s_cr_dve = sem("ctx_copied_by_dve")
        s_inv = sem("ctx_inverse_ready")
        s_cn = sem("ctx_normed")
        s_cz = sem("ctx_pad_zeroed")
        s_cout = [sem(f"ctx_written{i}") for i in range(2)]
        s_ctx = sem("ctx_loaded")
        s_wo = sem("out_product_done")
        s_u2 = sem("u2_ready")
        s_lgt_ps = sem("router_product_done")
        s_lgt = sem("router_rows_ready")
        s_lg_ps = sem("router_transposed")
        s_lg = sem("logits_ready")
        s_pexp = sem("router_exp_ready")
        s_mask = sem("mask_ready")
        s_pos = sem("positions_done")
        s_idx = sem("row_numbers_ready")
        s_zero = sem("zeros_ready")
        s_zfill = sem("scratch_zeroed")
        s_scat = sem("rows_scattered")
        s_xs0 = [sem(f"xs0_loaded{i}") for i in range(2)]
        s_w0 = [sem(f"w_l0_loaded{i}") for i in range(2)]
        s_xt_ps = sem("xs0_transposed")
        s_xt = sem("xs0_t_ready")
        s_h0_ps = sem("h0_product_done")
        s_h0 = sem("h0_ready")
        s_y0_ps = sem("y0_product_done")
        s_yt = sem("y0_t_ready")
        s_yo_ps = sem("y0_transposed")
        s_yo = sem("y0_ready")
        s_ys = [sem(f"ys0_written{i}") for i in range(2)]
        s_gz = sem("gather_zeroed")
        s_gath = sem("rows_gathered")
        s_x2 = sem("x2_ready")
        s_wal = sem("attn_weight_product_done")
        s_wal_sb = sem("attn_weight_ready")
        s_hg_ps = sem("graph_features_done")
        s_hg = sem("graph_features_ready")
        s_am = sem("max_column_ready")
        s_am_t = sem("max_column_transposed")
        s_am1 = sem("max_ready")
        s_am_bc = sem("max_broadcast")
        s_cexp = sem("factor_logs_ready")
        s_pqfg = sem("factors_ready")
        s_diag = sem("diagonals_ready")
        s_pqr = sem("factor_rows_done")
        s_pq_act = sem("factor_rows_by_act")
        s_pq_dve = sem("factor_rows_by_dve")
        s_adj1 = [sem(f"adj1_loaded{i}") for i in range(3)]
        s_t1 = sem("positive_branch_ready")
        s_t2 = sem("branches_maxed")
        s_w = sem("graph_weights_ready")
        s_g1 = sem("graph1_row_done")
        s_g1b = sem("graph1_rest_done")
        s_z = sem("graph1_normed")
        s_elu = sem("elu_min_ready")
        s_eexp = sem("elu_exp_ready")
        s_x3 = sem("x3_ready")
        s_w1 = sem("w_l1_loaded")
        s_scat1 = sem("rows_scattered1")
        s_te = sem("tile_experts_ready")
        s_x1l = sem("xs1_loaded")
        s_x1_ps = sem("xs1_transposed")
        s_x1t = sem("xs1_t_ready")
        s_h1_ps = sem("h1_product_done")
        s_h1pre = sem("h1_copied")
        s_h1t_ps = sem("h1_transposed")
        s_h1 = sem("h1_ready")
        s_y1_ps = sem("y1_product_done")
        s_y1 = sem("y1_ready")
        s_y1o = sem("ys1_written")
        s_combt_ps = sem("comb_transposed")
        s_combt = sem("comb_t_ready")
        s_b2 = sem("b2_products_done")
        s_gath1 = sem("rows_gathered1")
        s_fin = sem("output_ready")
        s_out = sem("output_written")

        s_b2_add = sem("b2_added")

        qk_chunks = [(hi_d, lo_d, mt, c) for hi_d, lo_d in ((q_hi_d, q_lo_d), (k_hi_d, k_lo_d))
                     for mt in range(DT) for c in range(QB)]
        w_l0_b2 = [w[:, B2AT:B2AT + DT] for w in w_l0]
        hg_flat = u_or_h[:, 0:T * D]
        UNITS = 2 * T
        CHUNKS = T * QB
        WTS = 16 * 7

        PRIMED = 1
        primed = [s_exp, s_av, s_cn, s_cr_act, s_cr_dve, *s_cout, s_h0, s_y0_ps, s_yt, s_yo_ps, s_yo, *s_ys,
                  s_g1, s_y1_ps, s_y1, s_y1o]

        block = ctx.enter_context(nc.Block())

        beside = {m: 4 for m in list(range(2, 11)) + [13, 14]}
        MT_AT = 16
        assert sum(beside.values()) == T * QB

        @block.sync
        def _(sp):
            sp.dma_start(x_res[:, :, :], a["x"].rearrange("(t p) d -> p t d", p=P)).then_inc(s_x, 16)
            sp.dma_start(const[:, :], a["const"]).then_inc(s_const, 16)
            sp.dma_start(rows[:, :, :].rearrange("p a d -> p (a d)"),
                         a["rows"].partition_broadcast(P)).then_inc(s_const, 16)
            adj = a["adj_t"].rearrange("(t p) n -> t p n", p=P)
            for j in range(3):
                sp.dma_start(adj0[j][:, :], adj[j]).then_inc(s_adj0[j], 16)
            for name, dst in (("vecs", vecs[:, :]), ("w_attn", w_attn[:, :, :, :]), ("w_graph", w_graph[:, :, 0:D]),
                              ("w_graph_t", w_graph_t[:, :, :]), ("attn_lr", attn_lr[:, :, :]),
                              ("w_router", w_router[:, :, :, :]), ("b2_l1", b2_l1[:, :])):
                sp.dma_start(dst, a[name]).then_inc(s_wts, 16)
            def load_row(slots, loaded, readers, j, k):
                sp.wait_ge(readers, j - 2)
                sp.dma_start(slots[k][:, :], adj[j]).then_inc(loaded[k], 16)

            with sp.Fori(0, (T - 3) // 3) as i:
                for k in range(3):
                    load_row(adj0, s_adj0, s_g0_row, i * 3 + (3 + k), k)
            for j in range(3 + (T - 3) // 3 * 3, T):
                load_row(adj0, s_adj0, s_g0_row, j, j % 3)
            sp.wait_ge(s_zero, 1)
            sp.dma_start(xs0_d.rearrange("(k p) d -> p k d", p=P),
                         zeros[:, None, :].to_broadcast([P, SLOTS0 // P, D])).then_inc(s_zfill, 16)
            sp.dma_start(xs1_d.rearrange("(k p) d -> p k d", p=P),
                         zeros[:, None, :].to_broadcast([P, TILES1, D])).then_inc(s_zfill, 16)
            sp.wait_ge(s_g0_row, T)
            for e in range(2):
                sp.dma_start(w_l0[e][:, :], a["w_l0"][e]).then_inc(s_w0[e], 16)
            for n, (hi_d, lo_d, mt, c) in enumerate(qk_chunks):
                there = (slice(mt * P, mt * P + P), slice(c * NC4, c * NC4 + NC4))
                sp.wait_ge(s_qk_hi, n + 1)
                sp.dma_start(hi_d[there], proj_hi[n % 2].bitcast(F32)[:, :]).then_inc(s_qk_out[n % 2], 16)
                sp.wait_ge(s_qk_lo, n + 1)
                sp.dma_start(lo_d[there], proj_lo[n % 2].bitcast(F32)[:, :]).then_inc(s_qk_out[n % 2], 16)
            for k in range(2):
                sp.wait_ge(s_qk_out[k], 16 * len(qk_chunks))

            def load_stack(k, h):
                for b, src in enumerate((q_hi_d, q_hi_d, q_lo_d)):
                    sp.dma_start(q_st[k].bitcast(F32)[b * DK:(b + 1) * DK, :],
                                 src[bass.ds(h * DK, DK), :]).then_inc(s_stack[k], 16)
                for b, src in enumerate((k_hi_d, k_lo_d, k_hi_d)):
                    sp.dma_start(k_st[k].bitcast(F32)[b * DK:(b + 1) * DK, :],
                                 src[bass.ds(h * DK, DK), :]).then_inc(s_stack[k], 16)

            def load_max(k, h):
                sp.wait_ge(s_mrow, h + 1)
                sp.dma_start(q_st[k].bitcast(F32)[3 * DK:3 * DK + 2, :].rearrange("c (t p) -> c t p", p=P),
                             m_rows.bitcast(F32)[:, :]).then_inc(s_mload[k], 16)

            load_stack(0, 0)
            load_stack(1, 1)
            load_max(0, 0)

            def heads(i, last):
                for k in range(2):
                    h = i * 2 + k
                    if not (last and k):
                        load_max(1 - k, h + 1)
                    if not last:
                        sp.wait_ge(s_s2, h * UNITS + UNITS)
                        load_stack(k, h + 2)
                    sp.wait_ge(s_cn, PRIMED + h * 2 + 2)
                    sp.dma_start(ctx_d[bass.ds(h * DK, DK), :], ctx_n[k][:, :]).then_inc(s_cout[k], 16)

            with sp.Fori(0, H // 2 - 1) as i:
                heads(i, False)
            heads(H // 2 - 1, True)
            for k in range(2):
                sp.wait_ge(s_cout[k], PRIMED + 16 * (H // 2))
            sp.dma_start(nt[:, :, :], ctx_d.rearrange("(c p) n -> p c n", p=P)).then_inc(s_ctx, 16)
            sp.dma_start(w_l1[:, E // 2:E, :], a["w_l1"][:, E // 2:E, :]).then_inc(s_w1, 16)

            def load_xs0(k, e):
                sp.dma_start(xs0[k][:, 0:CT - 1, :], xs0_d[bass.ds(e * CAPP, (CT - 1) * P), :]
                             .rearrange("(c p) d -> p c d", p=P)).then_inc(s_xs0[k], 16)
                sp.dma_start(xs0[k][0:CREM, CT - 1, :],
                             xs0_d[bass.ds(e * CAPP + (CT - 1) * P, CREM), :]).then_inc(s_xs0[k], 16)

            sp.wait_ge(s_scat, 16 * T)
            load_xs0(0, 0)
            load_xs0(1, 1)

            def experts(i, last):
                for k in range(2):
                    e = i * 2 + k
                    if not last:
                        sp.wait_ge(s_yt, PRIMED + e + 1)
                        sp.dma_start(w_l0[k][:, :], a["w_l0"][bass.ds(e + 2, 1), :, :]
                                     .rearrange("a p n -> p (a n)")).then_inc(s_w0[k], 16)
                        load_xs0(k, e + 2)
                    sp.wait_ge(s_yo, PRIMED + e + 1)
                    sp.dma_start(ys0_d[bass.ds(e * CAPP, (CT - 1) * P), :].rearrange("(c p) d -> p c d", p=P),
                                 y0[k][:, 0:CT - 1, :]).then_inc(s_ys[k], 16)
                    sp.dma_start(ys0_d[bass.ds(e * CAPP + (CT - 1) * P, CREM), :],
                                 y0[k][0:CREM, CT - 1, :]).then_inc(s_ys[k], 16)

            with sp.Fori(0, E // 2 - 1) as i:
                experts(i, False)
            experts(E // 2 - 1, True)

            sp.wait_ge(s_y0_ps, PRIMED + E)
            for j in range(3):
                sp.dma_start(adj1[j][:, :], adj[j]).then_inc(s_adj1[j], 16)
            with sp.Fori(0, (T - 3) // 3) as i:
                for k in range(3):
                    load_row(adj1, s_adj1, s_w, i * 3 + (3 + k), k)
            for j in range(3 + (T - 3) // 3 * 3, T):
                load_row(adj1, s_adj1, s_w, j, j % 3)
            sp.wait_ge(s_z, T)
            sp.dma_start(w_l1[:, 0:E // 2, :], a["w_l1"][:, 0:E // 2, :]).then_inc(s_w1, 16)

            sp.wait_ge(s_scat1, 2 * 16 * T)
            sp.dma_start(x1t[:, :], xs1_d[0:P, :]).then_inc(s_x1l, 16)
            sp.wait_ge(s_x1_ps, 1)
            sp.dma_start(x1t[:, :], xs1_d[P:2 * P, :]).then_inc(s_x1l, 16)
            sp.wait_ge(s_x1_ps, 2)
            sp.dma_start(x1t[:, :], xs1_d[2 * P:3 * P, :]).then_inc(s_x1l, 16)

            def store_y1(t):
                sp.wait_ge(s_y1, PRIMED + t + 1)
                sp.dma_start(ys1_d[bass.ds(t * P, P), :], y1t[:, :]).then_inc(s_y1o, 16)

            with sp.Fori(0, TILES1 - 3) as t:
                store_y1(t)
                sp.wait_ge(s_x1_ps, t + 3)
                sp.dma_start(x1t[:, :], xs1_d[bass.ds(t * P + 3 * P, P), :]).then_inc(s_x1l, 16)
            for t in range(TILES1 - 3, TILES1):
                store_y1(t)
            sp.wait_ge(s_fin, 1)
            sp.dma_start(out[0:(T - 1) * P, :].rearrange("(t p) d -> p t d", p=P),
                         x_res[:, 0:T - 1, :]).then_inc(s_out, 16)
            sp.dma_start(out[(T - 1) * P:N, :], x_res[0:LAST, T - 1, :]).then_inc(s_out, 16)
            sp.wait_ge(s_out, 32)

        @block.gpsimd
        def _(pool):
            for s in primed:
                pool.sem_inc(s, PRIMED)
            pool.memset(zeros[:, :], 0.0).then_inc(s_zero, 1)
            pool.memset(ones[:, :], 1.0).then_inc(s_ones, 1)
            pool.memset(v_nat[:, T - 1, :], 0.0).then_inc(s_vz, 1)
            for k in range(2):
                pool.memset(v_st[k][:, 0:T - 1, DK:2 * DK], 1.0).then_inc(s_vz, 1)
                pool.memset(v_st[k][:, T - 1, DK:2 * DK], 0.0).then_inc(s_vz, 1)
            pool.wait_ge(s_vz, 5)
            for k in range(2):
                pool.memset(v_st[k][0:LAST, T - 1, DK:2 * DK], 1.0).then_inc(s_vz, 1)
                pool.memset(k_st[k].bitcast(F32)[3 * DK:3 * DK + 2, :], 1.0).then_inc(s_kone, 1)
                pool.memset(ctx_n[k][:, 2 * HALF:NP], 0.0).then_inc(s_cz, 1)

            def stack_v(k, h):
                pool.tensor_copy(v_st[k][:, :, 0:DK], v_nat[:, :, bass.ds(h * DK, DK)]).then_inc(s_v_st, 1)

            pool.wait_ge(s_vz, 7)
            pool.wait_ge(s_kone, 2)
            pool.wait_ge(s_cz, 2)
            pool.wait_ge(s_v, T)
            for h in range(2):
                if h:
                    pool.wait_ge(s_v_st, h)
                stack_v(h, h)
            with pool.Fori(1, H // 2) as i:
                for k in range(2):
                    pool.wait_ge(s_av, PRIMED + i * (2 * UNITS) - (1 - k) * UNITS)
                    pool.wait_ge(s_v_st, i * 2 + k)
                    stack_v(k, i * 2 + k)

            pool.wait_ge(s_zfill, 32)
            pool.wait_ge(s_nat, 4)
            pool.wait_ge(s_idx, 1)
            for t in range(T):
                pool.indirect_dma_start(
                    out=xs0_d[:, :], out_offset=bass.IndirectOffsetOnAxis(ap=idx[:, 0, t:t + 1], axis=0),
                    in_=nat[:, t, :], in_offset=None, bounds_check=SLOTS0 - 1, oob_is_err=False).then_inc(s_scat, 16)
            pool.wait_ge(s_scat, 16 * T)
            pool.memset(nat[:, :, :], 0.0).then_inc(s_gz, 1)
            pool.wait_ge(s_gz, 1)
            for k in range(2):
                pool.wait_ge(s_ys[k], PRIMED + 32 * (E // 2))
            for t in range(T):
                pool.indirect_dma_start(
                    out=nat[:, t, :], out_offset=None, in_=ys0_d[:, :],
                    in_offset=bass.IndirectOffsetOnAxis(ap=idx[:, 0, t:t + 1], axis=0),
                    bounds_check=SLOTS0 - 1, oob_is_err=False).then_inc(s_gath, 16)

            pool.wait_ge(s_nat, 6)
            pool.wait_ge(s_idx, 3)
            for n in range(2):
                for t in range(T):
                    pool.indirect_dma_start(
                        out=xs1_d[:, :], out_offset=bass.IndirectOffsetOnAxis(ap=idx[:, n, t:t + 1], axis=0),
                        in_=nat[:, t, :], in_offset=None, bounds_check=SLOTS1 - 1,
                        oob_is_err=False).then_inc(s_scat1, 16)
            pool.wait_ge(s_scat1, 2 * 16 * T)
            pool.memset(nat[:, :, :], 0.0).then_inc(s_gz, 1)
            pool.memset(u[:, :, :], 0.0).then_inc(s_gz, 1)
            pool.wait_ge(s_gz, 3)
            pool.wait_ge(s_y1o, PRIMED + 16 * TILES1)
            for n, dst in enumerate((nat, u)):
                for t in range(T):
                    pool.indirect_dma_start(
                        out=dst[:, t, :], out_offset=None, in_=ys1_d[:, :],
                        in_offset=bass.IndirectOffsetOnAxis(ap=idx[:, n, t:t + 1], axis=0),
                        bounds_check=SLOTS1 - 1, oob_is_err=False).then_inc(s_gath1, 16)

        @block.scalar
        def _(act):
            def root(k):
                act.wait_ge(s_var, k)
                act.activation(std[:, :], var[:, :], ACT.Sqrt).then_inc(s_std, 1)

            def turned(r, g, b):
                for n in range(3):
                    lo, hi = 4 * n * P, min(4 * n + 4, T) * P
                    act.wait_ge(s_tr, 6 * r + 2 * n + 1)
                    if g is None:
                        act.activation(nt[:, 0, lo:hi], ps[:, 2 * n, 0:hi - lo], ACT.Identity).then_inc(s_tr_act, 1)
                    else:
                        act.activation(nt[:, 0, lo:hi], ps[:, 2 * n, 0:hi - lo], ACT.Identity,
                                       bias=vecs[:, b:b + 1], scale=vecs[:, g:g + 1]).then_inc(s_tr_act, 1)

            root(1)
            root(2)
            root(3)
            act.wait_ge(s_wts, WTS)
            turned(0, V_G1, V_B1)
            for n, (hi_d, lo_d, mt, c) in enumerate(qk_chunks):
                v = V_BQ if hi_d is q_hi_d else V_BK
                act.wait_ge(s_qk_ps, n + 1)
                if n >= 2:
                    act.wait_ge(s_qk_lo, n - 1)
                pads = v == V_BK and c == QB - 1
                real = N - c * NC4 if pads else NC4
                last = act.activation(proj[n % 2][:, 0:real], ps[:, n % 8, 0:real], ACT.Identity,
                                      bias=vecs[:, v + mt:v + mt + 1])
                if pads:
                    last = act.activation(proj[n % 2][:, real:NC4], ps[:, (n - c) % 8, 0:NC4 - real], ACT.Identity,
                                          bias=vecs[:, v + mt:v + mt + 1])
                last.then_inc(s_qk_raw, 1)

            def head(h):
                for m in range(UNITS):
                    act.wait_ge(s_s2, h * UNITS + (m + 1))
                    act.wait_ge(s_av, PRIMED + h * UNITS + max(m - 1, 0))
                    act.activation(expo[m % 2][:, :].rearrange("p (c q) -> p c q", c=2),
                                   ps[:, 2 + 2 * (m % 2):4 + 2 * (m % 2), 0:QC], ACT.Exp,
                                   scale=SCALE).then_inc(s_exp, 1)
                    if m == T or m == UNITS - 1:
                        half = m // T if m == UNITS - 1 else 0
                        act.wait_ge(s_av, PRIMED + h * UNITS + T * (half + 1))
                        act.wait_ge(s_cn, PRIMED + h * 2)
                        act.copy(ctx_raw[half][:, 0:QC], ps[0:2 * DK, 6, 0:QC]).then_inc(s_cr_act, 1)

            with act.Fori(0, H) as h:
                head(h)

            root(4)
            turned(1, V_G2, V_B2)
            act.wait_ge(s_lg, 2)
            act.activation(probs[:, :, :], lg[:, :, :], ACT.Exp).then_inc(s_pexp, 1)

            def expert0(i, k):
                e = i * 2 + k
                act.wait_ge(s_w0[k], i * 16 + 16)
                for f in range(FT):
                    act.wait_ge(s_h0_ps, e * FT + (f + 1))
                    if f == 0:
                        act.wait_ge(s_y0_ps, PRIMED + e)
                    act.activation(h0[:, f, :], ps[:, 2 + f % 2, 0:CAPP], ACT.Gelu,
                                   bias=w_l0[k][:, B1AT + f:B1AT + f + 1]).then_inc(s_h0, 1)

            with act.Fori(0, E // 2) as i:
                expert0(i, 0)
                expert0(i, 1)

            root(5)
            turned(2, None, None)
            for t in range(T):
                act.wait_ge(s_hg_ps, t + 1)
                act.copy(hg[:, t, 0:D], ps[:, t % 8, 0:D])
                act.copy(a12[:, t, :], ps[:, t % 8, D:D + 2]).then_inc(s_hg, 1)
            act.wait_ge(s_cexp, 1)
            act.activation(pq[:, 0, :], cneg[:, :], ACT.Exp, scale=0.8)
            act.activation(pq[:, 1, :], cpos[:, :], ACT.Exp, scale=-0.8)
            act.activation(fg[:, 0, :], agap[:, :], ACT.Exp)
            act.activation(fg[:, 1, :], agap[:, :], ACT.Exp, scale=0.2).then_inc(s_pqfg, 1)
            for n in range(3):
                lo, hi = 4 * n * P, min(4 * n + 4, T) * P
                act.wait_ge(s_pqr, 2 * n + 1)
                act.copy(pq_rows[:, 0, lo:hi], ps[:, 2 * n, 0:hi - lo]).then_inc(s_pq_act, 1)
            act.wait_ge(s_pq_act, 3)

            def positive(j, k):
                act.activation(wgt[k][:, :], pq_rows[:, 0, :], ACT.Identity,
                               scale=fg[:, 0, bass.ds(j, 1)]).then_inc(s_t1, 1)

            act.wait_ge(s_pqfg, 1)
            for j in range(2):
                positive(j, j)
            with act.Fori(0, 3) as i:
                for k in range(3):
                    act.wait_ge(s_g1, PRIMED + i * 3 + k)
                    positive(i * 3 + (2 + k), (2 + k) % 3)
            for n in range(2):
                act.wait_ge(s_elu, n + 1)
                lo, hi = ((0, GA), (GA, T))[n]
                act.activation(hg_flat[:, lo * D:hi * D], hg_flat[:, lo * D:hi * D], ACT.Exp).then_inc(s_eexp, 1)

            root(6)
            turned(3, None, None)
            act.wait_ge(s_lg, 4)
            act.activation(probs[:, :, :], lg[:, :, :], ACT.Exp).then_inc(s_pexp, 1)
            act.wait_ge(s_te, 1)
            act.wait_ge(s_w1, 32)

            def gelu1(t):
                e = act.value_load(tile_expert[0:1, bass.ds(t, 1)], min_val=0, max_val=E - 1)
                act.wait_ge(s_h1t_ps, t + 1)
                act.wait_ge(s_y1_ps, PRIMED + t)
                for f in range(FT):
                    last = act.activation(h1[:, f, :], ps[:, 4 + f // 4, (f % 4) * P:(f % 4 + 1) * P],
                                          ACT.Gelu_apprx_tanh, bias=w_l1[:, bass.ds(e, 1), B1AT + f])
                last.then_inc(s_h1, 1)

            with act.Fori(0, TILES1) as t:
                gelu1(t)

        @block.tensor
        def _(pe):
            def turn(r, k):
                pe.wait_ge(s_nat, k)
                for n in range(3):
                    for c in range(DT):
                        for t in range(4 * n, min(4 * n + 4, T)):
                            last = pe.transpose(ps[:, 2 * n + c, (t - 4 * n) * P:(t - 4 * n + 1) * P],
                                                nat[:, t, c * P:(c + 1) * P], ident)
                        last.then_inc(s_tr, 1)

            def turned(r):
                pe.wait_ge(s_tr_act, 3 * r + 3)
                pe.wait_ge(s_tr_dve, 3 * r + 3)

            def graph0(j, k, first, last):
                for t in range(T):
                    mm = pe.matmul(ps[:, t // 2, (t % 2) * D:(t % 2 + 1) * D], adj0[k][:, t * P:(t + 1) * P],
                                   nat[:, j, :] if first else nat[:, bass.ds(j, 1), :].rearrange("p a d -> p (a d)"),
                                   start=first and t % 2 == 0, stop=last, skip_group_check=True)
                mm.then_inc(s_g0_row, 1)

            pe.wait_ge(s_hid, 1)
            for j in range(2):
                pe.wait_ge(s_adj0[j], 16)
                graph0(j, j, j == 0, False)
            with pe.Fori(0, 3) as i:
                for k in range(3):
                    pe.wait_ge(s_adj0[(2 + k) % 3], i * 16 + (16 if k == 0 else 32))
                    graph0(i * 3 + (2 + k), (2 + k) % 3, False, False)

            pe.wait_ge(s_const, 32)
            turn(0, 3)
            turned(0)
            pe.wait_ge(s_wts, WTS)
            for n, (hi_d, lo_d, mt, c) in enumerate(qk_chunks):
                w = w_attn[:, 0 if hi_d is q_hi_d else 1, :, :]
                if n >= 8:
                    pe.wait_ge(s_qk_raw, 4 * ((n - 8) // 4) + 4)
                for kt in range(DT):
                    mm = pe.matmul(ps[:, n % 8, 0:NC4], w[:, kt, mt * P:(mt + 1) * P],
                                   nt[:, kt, c * NC4:(c + 1) * NC4], start=kt == 0, stop=kt == DT - 1)
                mm.then_inc(s_qk_ps, 1)
            for t in range(T):
                if t < 8:
                    pe.wait_ge(s_qk_raw, 8 + 4 * (t // 4) + 4)
                else:
                    pe.wait_ge(s_v, t - 7)
                for kt in range(DT):
                    mm = pe.matmul(ps[:, t % 8, 0:D], nt[:, kt, t * P:(t + 1) * P], w_attn[:, 2, kt, :],
                                   start=kt == 0, stop=kt == DT - 1)
                mm.then_inc(s_v_ps, 1)

            def max_chunk(h, k, n, free):
                if free:
                    pe.wait_ge(s_mx, h * CHUNKS + (n - 1))
                pe.matmul(ps[:, n % 2, 0:QC], q_st[k][0:3 * DK, (n // QB) * P:(n // QB + 1) * P],
                          k_st[k][0:3 * DK, (n % QB) * QC:(n % QB + 1) * QC],
                          start=True, stop=True).then_inc(s_s1, 1)

            def max_rows(h):
                pe.wait_ge(s_hl, h + 1)
                pe.transpose(ps[0:2 * T, 0, 0:P], m_hl.bitcast(F32)[:, :], ident).then_inc(s_mt, 1)

            def scores(h, k, m):
                pe.wait_ge(s_exp, PRIMED + h * UNITS + max(m - 1, 0))
                half, kt = m // T, m % T
                for c in range(2):
                    at = half * HALF + c * QC
                    mm = pe.matmul(ps[:, 2 + 2 * (m % 2) + c, 0:QC], k_st[k][0:3 * DK + 2, kt * P:(kt + 1) * P],
                                   q_st[k][0:3 * DK + 2, at:at + QC], start=True, stop=True)
                mm.then_inc(s_s2, 1)

            def values(h, k, m):
                half, kt = m // T, m % T
                if kt == 0:
                    pe.wait_ge(s_cr_act, PRIMED + h * 2 + half)
                    pe.wait_ge(s_cr_dve, PRIMED + h * 2 + half)
                pe.wait_ge(s_exp, PRIMED + h * UNITS + (m + 1))
                for c in range(2):
                    mm = pe.matmul(ps[0:2 * DK, 6 + c, 0:QC], v_st[k][:, kt, :], expo[m % 2][:, c * QC:(c + 1) * QC],
                                   start=kt == 0, stop=kt == T - 1)
                mm.then_inc(s_av, 1)

            def head(i, k, more):
                h = i * 2 + k
                pe.wait_ge(s_v_st, h + 1)
                pe.wait_ge(s_mload[k], i * 16 + 16)
                scores(h, k, 0)
                n = 0
                for m in range(UNITS):
                    if m < UNITS - 1:
                        scores(h, k, m + 1)
                    if more and m in beside:
                        if n == 0:
                            pe.wait_ge(s_stack[1 - k], i * 96 + (96 if k == 0 else 192))
                            pe.wait_ge(s_mrow, h + 1)
                        for _ in range(beside[m]):
                            max_chunk(h + 1, 1 - k, n, True)
                            n += 1
                    if more and m == MT_AT:
                        max_rows(h + 1)
                    values(h, k, m)

            pe.wait_ge(s_v, T)
            pe.wait_ge(s_kone, 2)
            pe.wait_ge(s_vz, 7)
            pe.wait_ge(s_stack[0], 96)
            for n in range(CHUNKS):
                max_chunk(0, 0, n, n >= 2)
            max_rows(0)
            with pe.Fori(0, H // 2 - 1) as i:
                head(i, 0, True)
                head(i, 1, True)
            head(H // 2 - 1, 0, True)
            head(H // 2 - 1, 1, False)

            pe.wait_ge(s_ctx, 16)
            for t in range(T):
                if t >= 8:
                    pe.wait_ge(s_u2, t - 7)
                for kt in range(DT):
                    mm = pe.matmul(ps[:, t % 8, 0:D], nt[:, kt, t * P:(t + 1) * P], w_attn[:, 3, kt, :],
                                   start=kt == 0, stop=kt == DT - 1)
                mm.then_inc(s_wo, 1)

            def route(layer):
                for c in range(QB):
                    for kt in range(DT):
                        mm = pe.matmul(ps[0:E, 2 + c, 0:NC4], w_router[:, layer, kt, :],
                                       nt[:, kt, c * NC4:(c + 1) * NC4], start=kt == 0, stop=kt == DT - 1)
                mm.then_inc(s_lgt_ps, 1)
                pe.wait_ge(s_lgt, layer + 1)
                for t in range(T):
                    mm = pe.transpose(ps[:, 6, t * E:(t + 1) * E], lgt[:, t * P:(t + 1) * P], const[0:E, C_ID:C_ID + E])
                mm.then_inc(s_lg_ps, 1)
                pe.wait_ge(s_mask, layer + 1)
                pe.matmul(ps[:, 7, 0:T * E], tri_b[:, :], mask_b[:, :, :].rearrange("p t e -> p (t e)"),
                          start=True, stop=False, skip_group_check=True)
                for t in range(T - 1):
                    mm = pe.matmul(ps[:, 7, (t + 1) * E:T * E].rearrange("p (t e) -> p t e", e=E), ones_b[:, :],
                                   mask_b[:, t:t + 1, :].to_broadcast([P, T - 1 - t, E]),
                                   start=False, stop=t == T - 2, skip_group_check=True)
                if layer:
                    for t in range(T):
                        mm = pe.matmul(ps[:, 0, 0:E], ones_b[:, :], mask_b[:, t, :], start=t == 0, stop=t == T - 1)
                mm.then_inc(s_pos, 1)

            turn(1, 4)
            turned(1)
            route(0)

            def xs_in(k, e, need):
                pe.wait_ge(s_xs0[k], need)
                pe.wait_ge(s_xt, e)
                for c in range(DT):
                    for s in range(CT):
                        w = P if s < CT - 1 else CREM
                        mm = pe.transpose(ps[:, c, s * P:s * P + w], xs0[k][0:w, s, c * P:(c + 1) * P],
                                          const[0:w, C_ID:C_ID + w])
                mm.then_inc(s_xt_ps, 1)

            def expert0(i, k, more):
                e = i * 2 + k
                pe.wait_ge(s_w0[k], i * 16 + 16)
                pe.wait_ge(s_xt, e + 1)
                for f in range(FT):
                    pe.wait_ge(s_h0, PRIMED + e * FT + max(f - 1, 0))
                    for kt in range(DT):
                        mm = pe.matmul(ps[:, 2 + f % 2, 0:CAPP], w_l0[k][:, kt * F + f * P:kt * F + (f + 1) * P],
                                       xs0_t[:, kt, :], start=kt == 0, stop=kt == DT - 1)
                    mm.then_inc(s_h0_ps, 1)
                pe.wait_ge(s_yt, PRIMED + e)
                for c in range(DT):
                    for f in range(FT):
                        if c == 0:
                            pe.wait_ge(s_h0, PRIMED + e * FT + (f + 1))
                        at = DT * F + f * D + c * P
                        mm = pe.matmul(ps[:, 4 + c, 0:CAPP], w_l0[k][:, at:at + P], h0[:, f, :],
                                       start=f == 0, stop=f == FT - 1)
                mm.then_inc(s_y0_ps, 1)
                if more:
                    xs_in(1 - k, e + 1, i * 32 + (32 if k == 0 else 64))
                pe.wait_ge(s_yt, PRIMED + e + 1)
                pe.wait_ge(s_yo, PRIMED + e)
                for s in range(CT):
                    w = P if s < CT - 1 else CREM
                    for c in range(DT):
                        mm = pe.transpose(ps[0:w, 6 + s // 2, (s % 2) * D + c * P:(s % 2) * D + (c + 1) * P],
                                          y0_t[:, c, s * P:s * P + w], ident)
                mm.then_inc(s_yo_ps, 1)

            xs_in(0, 0, 32)
            with pe.Fori(0, E // 2 - 1) as i:
                expert0(i, 0, True)
                expert0(i, 1, True)
            expert0(E // 2 - 1, 0, True)
            expert0(E // 2 - 1, 1, False)

            for c in range(DT):
                for kt in range(DT):
                    mm = pe.matmul(ps[:, 2, 2 * c:2 * c + 2], w_graph_t[:, kt, c * P:(c + 1) * P], attn_lr[:, kt, :],
                                   start=kt == 0, stop=kt == DT - 1)
            mm.then_inc(s_wal, 1)
            turn(2, 5)
            turned(2)
            pe.wait_ge(s_wal_sb, 1)
            for t in range(T):
                if t >= 8:
                    pe.wait_ge(s_hg, t - 7)
                for kt in range(DT):
                    mm = pe.matmul(ps[:, t % 8, 0:D + 2], nt[:, kt, t * P:(t + 1) * P], w_graph[:, kt, :],
                                   start=kt == 0, stop=kt == DT - 1)
                mm.then_inc(s_hg_ps, 1)
            pe.wait_ge(s_am, 1)
            pe.transpose(ps[0:1, 7, 0:P], a_max[:, :], ident).then_inc(s_am_t, 1)
            pe.wait_ge(s_am1, 1)
            pe.matmul(ps[:, 6, 0:1], ones[0:1, :], a_max1[:, :], start=True, stop=True).then_inc(s_am_bc, 1)
            pe.wait_ge(s_diag, 2)
            for n in range(3):
                w = (min(4 * n + 4, T) - 4 * n) * P
                for c in range(2):
                    at = c * T + 4 * n
                    pe.matmul(ps[:, 2 * n + c, 0:w], ones[:, :],
                              diag[:, at:at + w // P, :], start=True, stop=True).then_inc(s_pqr, 1)
            pe.wait_ge(s_hg, T)

            def graph1(j, k, first):
                for t in range(GA):
                    mm = pe.matmul(ps[:, t, 0:D + 2], wgt[k][:, t * P:(t + 1) * P],
                                   hg[:, j, :] if first else hg[:, bass.ds(j, 1), :].rearrange("p a d -> p (a d)"),
                                   start=first, stop=False, skip_group_check=True)
                mm.then_inc(s_g1, 1)

            for j in range(2):
                pe.wait_ge(s_w, j + 1)
                graph1(j, j, j == 0)
            with pe.Fori(0, 3) as i:
                for k in range(3):
                    pe.wait_ge(s_w, i * 3 + (3 + k))
                    graph1(i * 3 + (2 + k), (2 + k) % 3, False)
            pe.wait_ge(s_z, GB)
            for t in range(GB):
                for j in range(T):
                    mm = pe.matmul(ps[:, t, 0:D + 2], wgt_keep[:, j, t * P:(t + 1) * P], hg[:, j, :],
                                   start=j == 0, stop=j == T - 1)
                mm.then_inc(s_g1b, 1)

            turn(3, 6)
            turned(3)
            route(1)
            pe.wait_ge(s_idx, 3)
            for t in range(T):
                mm = pe.transpose(ps[0:E, t // 4, (t % 4) * P:(t % 4 + 1) * P], comb[:, t, :], ident)
            mm.then_inc(s_combt_ps, 1)
            pe.wait_ge(s_combt, 1)
            for t in range(T):
                if t >= 6:
                    pe.wait_ge(s_b2_add, t - 5)
                pe.matmul(ps[:, 2 + t % 6, 0:D], comb_t[:, t * P:(t + 1) * P], b2_l1[:, :],
                          start=True, stop=True).then_inc(s_b2, 1)
            pe.wait_ge(s_b2_add, T)
            pe.wait_ge(s_w1, 32)
            pe.wait_ge(s_te, 1)

            def xs1_in(t):
                pe.wait_ge(s_x1l, t * 16 + 16)
                pe.wait_ge(s_x1t, t)
                for c in range(DT):
                    mm = pe.transpose(ps[:, 0, c * P:(c + 1) * P], x1t[:, c * P:(c + 1) * P], ident)
                mm.then_inc(s_x1_ps, 1)

            def up1(t):
                e = pe.value_load(tile_expert[0:1, bass.ds(t, 1)], min_val=0, max_val=E - 1)
                pe.wait_ge(s_x1t, t + 1)
                pe.wait_ge(s_h1pre, t)
                for b in range(2):
                    for kt in range(DT):
                        at = kt * F + b * 512
                        mm = pe.matmul(ps[:, 2 + b, :], x1t_t[:, kt, :],
                                       w_l1[:, bass.ds(e, 1), at:at + 512].rearrange("p a n -> p (a n)"),
                                       start=kt == 0, stop=kt == DT - 1)
                mm.then_inc(s_h1_ps, 1)

            def h1_turn(t):
                pe.wait_ge(s_h1pre, t + 1)
                pe.wait_ge(s_h1, t)
                for f in range(FT):
                    mm = pe.transpose(ps[:, 4 + f // 4, (f % 4) * P:(f % 4 + 1) * P], h1pre[:, f * P:(f + 1) * P], ident)
                mm.then_inc(s_h1t_ps, 1)

            def down1(t):
                e = pe.value_load(tile_expert[0:1, bass.ds(t, 1)], min_val=0, max_val=E - 1)
                pe.wait_ge(s_h1, t + 1)
                pe.wait_ge(s_y1, PRIMED + t)
                for f in range(FT):
                    at = DT * F + f * D
                    mm = pe.matmul(ps[:, 6, 0:D], h1[:, f, :],
                                   w_l1[:, bass.ds(e, 1), at:at + D].rearrange("p a n -> p (a n)"),
                                   start=f == 0, stop=f == FT - 1)
                mm.then_inc(s_y1_ps, 1)

            xs1_in(0)
            up1(0)
            h1_turn(0)
            xs1_in(1)
            with pe.Fori(0, TILES1 - 2) as t:
                up1(t + 1)
                down1(t)
                h1_turn(t + 1)
                xs1_in(t + 2)
            up1(TILES1 - 1)
            down1(TILES1 - 2)
            h1_turn(TILES1 - 1)
            down1(TILES1 - 1)

        @block.vector
        def _(dve):
            steps = [0]

            def step(ins):
                steps[0] += 1
                ins.then_inc(s_step, 1)
                dve.wait_ge(s_step, steps[0])

            def norm(k, src, dst):
                for t in range(T):
                    last = dve.bn_stats(stats[:, t, :], src[:, t, :])
                step(last)
                for t in range(T):
                    last = dve.bn_aggr(mv[:, t, :], stats[:, t, :])
                step(last)
                dve.tensor_scalar(var[:, :], mv[:, :, 1], EPS, None, ALU.add).then_inc(s_var, 1)
                dve.wait_ge(s_std, k)
                step(dve.reciprocal(rstd[:, :], std[:, :]))
                for t in range(T):
                    last = dve.tensor_scalar(dst[:, t, :], src[:, t, :], mv[:, t, 0:1], rstd[:, t:t + 1],
                                             ALU.subtract, ALU.mult)
                return last

            def turned(r, g, b):
                for n in range(3):
                    lo, hi = 4 * n * P, min(4 * n + 4, T) * P
                    dve.wait_ge(s_tr, 6 * r + 2 * n + 2)
                    src = ps[:, 2 * n + 1, 0:hi - lo]
                    if g is None:
                        dve.tensor_copy(nt[:, 1, lo:hi], src).then_inc(s_tr_dve, 1)
                    else:
                        dve.tensor_scalar(nt[:, 1, lo:hi], src, vecs[:, g + 1:g + 2], vecs[:, b + 1:b + 2],
                                          ALU.mult, ALU.add).then_inc(s_tr_dve, 1)

            dve.wait_ge(s_x, 16)
            step(norm(1, x_res, nat))
            dve.wait_ge(s_const, 32)
            dve.tensor_tensor(nat[:, :, :], nat[:, :, :], rows[:, 2:3, :].to_broadcast([P, T, D]),
                              ALU.mult).then_inc(s_hid, 1)
            dve.tensor_copy(tri_b[:, :], const[:, C_TRI:C_TRI + P])
            dve.wait_ge(s_ones, 1)
            dve.tensor_copy(ones_b[:, :], ones[:, :])
            dve.wait_ge(s_g0_row, T)
            for b in range(6):
                w = min(2, T - 2 * b)
                last = dve.tensor_tensor(x_res[:, 2 * b:2 * b + w, :], x_res[:, 2 * b:2 * b + w, :],
                                         ps[:, b, 0:w * D].rearrange("p (t d) -> p t d", d=D), ALU.add)
            step(last)

            step(norm(2, x_res, u))
            norm(3, u, nat).then_inc(s_nat, 3)
            dve.wait_ge(s_wts, WTS)
            turned(0, V_G1, V_B1)
            for n in range(len(qk_chunks)):
                dve.wait_ge(s_qk_raw, n + 1)
                if n >= 2:
                    dve.wait_ge(s_qk_out[n % 2], 32 * (n // 2))
                dve.tensor_copy(proj_hi[n % 2][:, :], proj[n % 2][:, :]).then_inc(s_qk_hi, 1)
                dve.wait_ge(s_qk_hi, n + 1)
                dve.tensor_tensor(proj_lo[n % 2][:, :], proj[n % 2][:, :], proj_hi[n % 2].bitcast(F32)[:, :],
                                  ALU.subtract).then_inc(s_qk_lo, 1)
            dve.wait_ge(s_vz, 1)
            for t in range(T):
                w = P if t < T - 1 else LAST
                dve.wait_ge(s_v_ps, t + 1)
                dve.tensor_tensor(v_nat[0:w, t, :], ps[0:w, t % 8, 0:D], rows[0:w, 0, :], ALU.add).then_inc(s_v, 1)

            def chunk_max(h, n):
                dve.wait_ge(s_s1, h * CHUNKS + (n + 1))
                dve.tensor_reduce(mx4[:, n // QB, n % QB:n % QB + 1], ps[:, n % 2, 0:QC], AX_X, ALU.max).then_inc(s_mx, 1)

            def neg_max(h):
                dve.wait_ge(s_mx, (h + 1) * CHUNKS)
                dve.tensor_reduce(negm[:, :], mx4[:, :, :], AX_X, ALU.max).then_inc(s_mq, 1)
                dve.wait_ge(s_mq, h * 3 + 1)
                dve.tensor_scalar(negm[:, :], negm[:, :], -1.0, None, ALU.mult).then_inc(s_mq, 1)
                dve.wait_ge(s_mt, h)
                dve.wait_ge(s_mq, h * 3 + 2)
                dve.tensor_copy(m_hl[:, 0:T], negm[:, :]).then_inc(s_mq, 1)
                dve.wait_ge(s_mq, h * 3 + 3)
                dve.tensor_tensor(m_hl[:, T:2 * T], negm[:, :], m_hl.bitcast(F32)[:, 0:T],
                                  ALU.subtract).then_inc(s_hl, 1)

            def copy_half(h, half):
                dve.wait_ge(s_av, PRIMED + h * UNITS + T * (half + 1))
                dve.wait_ge(s_cn, PRIMED + h * 2)
                dve.tensor_copy(ctx_raw[half][:, QC:HALF], ps[0:2 * DK, 7, 0:QC]).then_inc(s_cr_dve, 1)

            def norm_half(h, i, k, half):
                dve.wait_ge(s_cr_act, PRIMED + h * 2 + (half + 1))
                dve.wait_ge(s_cr_dve, PRIMED + h * 2 + (half + 1))
                dve.reciprocal(ctx_inv[:, :], ctx_raw[half][DK:2 * DK, :]).then_inc(s_inv, 1)
                dve.wait_ge(s_inv, h * 2 + (half + 1))
                dve.wait_ge(s_cout[k], PRIMED + i * 16)
                dve.tensor_tensor(ctx_n[k][:, half * HALF:(half + 1) * HALF], ctx_raw[half][0:DK, :], ctx_inv[:, :],
                                  ALU.mult).then_inc(s_cn, 1)

            def head(i, k, more):
                h = i * 2 + k
                n = 0
                for m in range(UNITS):
                    if m == T:
                        copy_half(h, 0)
                    if m == T + 1:
                        norm_half(h, i, k, 0)
                    if more and m in beside:
                        for _ in range(beside[m]):
                            chunk_max(h + 1, n)
                            n += 1
                        if n == CHUNKS:
                            neg_max(h + 1)
                    if more and m == MT_AT:
                        dve.wait_ge(s_mt, h + 2)
                        dve.wait_ge(s_mload[k], i * 16 + 16)
                        dve.tensor_copy(m_rows[:, :], ps[0:2 * T, 0, 0:P]).then_inc(s_mrow, 1)
                copy_half(h, 1)
                norm_half(h, i, k, 1)

            for n in range(CHUNKS):
                chunk_max(0, n)
            neg_max(0)
            dve.wait_ge(s_mt, 1)
            dve.tensor_copy(m_rows[:, :], ps[0:2 * T, 0, 0:P]).then_inc(s_mrow, 1)
            step(dve.tensor_tensor(u[:, :, :], u[:, :, :], rows[:, 1:2, :].to_broadcast([P, T, D]), ALU.add))
            dve.wait_ge(s_cz, 2)
            with dve.Fori(0, H // 2 - 1) as i:
                head(i, 0, True)
                head(i, 1, True)
            head(H // 2 - 1, 0, True)
            head(H // 2 - 1, 1, False)

            for t in range(T):
                dve.wait_ge(s_wo, t + 1)
                dve.tensor_tensor(u[:, t, :], u[:, t, :], ps[:, t % 8, 0:D], ALU.add).then_inc(s_u2, 1)
            dve.wait_ge(s_u2, T)
            norm(4, u, nat).then_inc(s_nat, 1)
            dve.tensor_tensor(x_res[:, :, :], x_res[:, :, :], u[:, :, :], ALU.add)
            turned(1, V_G2, V_B2)

            def over_e(v):
                return v[:, :, None].to_broadcast([P, T, E])

            def choose(layer):
                dve.wait_ge(s_lgt_ps, layer + 1)
                dve.tensor_scalar(lgt[:, :].rearrange("e (c n) -> e c n", c=QB), ps[0:E, 2:6, 0:NC4],
                                  vecs[0:E, V_RB + layer:V_RB + layer + 1], None, ALU.add).then_inc(s_lgt, 1)
                dve.wait_ge(s_lg_ps, layer + 1)
                dve.tensor_copy(lg[:, :, :], ps[:, 6, 0:T * E].rearrange("p (t e) -> p t e", e=E)).then_inc(s_lg, 1)
                dve.wait_ge(s_lg, 2 * layer + 1)
                step(dve.tensor_reduce(top1[:, :], lg[:, :, :], AX_X, ALU.max))
                step(dve.tensor_tensor(lg[:, :, :], lg[:, :, :], over_e(top1), ALU.subtract))
                dve.tensor_scalar(lg[:, :, :], lg[:, :, :], UNDER, None, ALU.max).then_inc(s_lg, 1)
                dve.wait_ge(s_lg, 2 * layer + 2)
                lj = lg[:, :, :, None].to_broadcast([P, T, E, E])
                li = lg[:, :, None, :].to_broadcast([P, T, E, E])
                dve.tensor_tensor(cmp_gt[:, :, :, :], lj, li, ALU.is_gt)
                step(dve.tensor_tensor(cmp_eq[:, :, :, :], lj, li, ALU.is_equal))
                lower = const[:, C_LT:C_LT + E * E].rearrange("p (o n) -> p o n", o=1).to_broadcast([P, T, E * E])
                eq = cmp_eq[:, :, :, :].rearrange("p t j i -> p t (j i)")
                step(dve.tensor_tensor(eq, eq, lower, ALU.mult))
                step(dve.tensor_tensor(cmp_gt[:, :, :, :], cmp_gt[:, :, :, :], cmp_eq[:, :, :, :], ALU.add))
                step(dve.tensor_reduce(mask[:, :, :], cmp_gt[:, :, :, :].rearrange("p t j i -> p t i j"), AX_X, ALU.add))
                step(dve.tensor_scalar(mask[:, :, :], mask[:, :, :], 1.5, None, ALU.is_lt))
                step(dve.tensor_tensor(mask[:, :, :], mask[:, :, :], over_e(valid), ALU.mult))
                dve.tensor_copy(mask_b[:, :, :], mask[:, :, :]).then_inc(s_mask, 1)

            def row_number(dst, n):
                step(dve.tensor_scalar(skip[:, :], dst[:, :], 0.0, FAR, ALU.is_equal, ALU.mult))
                step(dve.tensor_tensor(skip[:, :], skip[:, :], dst[:, :], ALU.add))
                dve.tensor_scalar(idx[:, n, :], skip[:, :], -1.0, None, ALU.add).then_inc(s_idx, 1)

            choose(0)
            dve.wait_ge(s_pos, 1)
            pos = ps[:, 7, 0:T * E].rearrange("p (t e) -> p t e", e=E)
            off = const[:, C_OFF:C_OFF + E].rearrange("p (o e) -> p o e", o=1).to_broadcast([P, T, E])
            step(dve.tensor_scalar(slot[:, :, :], pos, CAP - 0.5, None, ALU.is_lt))
            step(dve.tensor_tensor(mask[:, :, :], mask[:, :, :], slot[:, :, :], ALU.mult))
            step(dve.tensor_tensor(slot[:, :, :], pos, off, ALU.add))
            step(dve.tensor_tensor(slot[:, :, :], slot[:, :, :], mask[:, :, :], ALU.mult))
            step(dve.tensor_reduce(sa[:, :], slot[:, :, :], AX_X, ALU.max))
            row_number(sa, 0)

            def xs_t(e):
                dve.wait_ge(s_xt_ps, e + 1)
                for c in range(DT):
                    last = dve.tensor_scalar(xs0_t[:, c, :], ps[:, c, 0:CAPP], vecs[:, V_G2 + c:V_G2 + c + 1],
                                             vecs[:, V_B2 + c:V_B2 + c + 1], ALU.mult, ALU.add)
                last.then_inc(s_xt, 1)

            def expert0(i, k, more):
                e = i * 2 + k
                dve.wait_ge(s_y0_ps, PRIMED + e + 1)
                dve.wait_ge(s_yo_ps, PRIMED + e)
                for c in range(DT):
                    last = dve.tensor_scalar(y0_t[:, c, :], ps[:, 4 + c, 0:CAPP], w_l0_b2[k][:, c:c + 1], None, ALU.add)
                last.then_inc(s_yt, 1)
                if more:
                    xs_t(e + 1)
                dve.wait_ge(s_yo_ps, PRIMED + e + 1)
                dve.wait_ge(s_ys[k], PRIMED + i * 32)
                dve.tensor_copy(y0[k][:, 0:2, :], ps[:, 6, :].rearrange("p (s d) -> p s d", d=D))
                dve.tensor_copy(y0[k][0:CREM, 2, :], ps[0:CREM, 7, 0:D]).then_inc(s_yo, 1)

            xs_t(0)
            with dve.Fori(0, E // 2 - 1) as i:
                expert0(i, 0, True)
                expert0(i, 1, True)
            expert0(E // 2 - 1, 0, True)
            expert0(E // 2 - 1, 1, False)
            dve.wait_ge(s_wal, 1)
            dve.tensor_copy(w_graph[:, :, D:D + 2], ps[:, 2, 0:2 * DT].rearrange("p (c n) -> p c n", n=2)).then_inc(s_wal_sb, 1)
            dve.wait_ge(s_gath, 16 * T)
            step(dve.tensor_tensor(x_res[:, :, :], x_res[:, :, :], nat[:, :, :], ALU.add))

            step(norm(5, x_res, nat))
            dve.tensor_scalar(nat[:, T - 1, :], nat[:, T - 1, :], valid[:, T - 1:T], None, ALU.mult).then_inc(s_nat, 1)
            dve.memset(hg[:, :, D:D + 1], 1.0)
            dve.memset(hg[:, :, D + 1:D + 2], 0.0)
            turned(2, None, None)
            dve.wait_ge(s_hg, T)
            step(dve.tensor_scalar(a_all[:, :], valid[:, T - 1:T], 1.0, 1.0e30, ALU.subtract, ALU.mult))
            step(dve.tensor_tensor(a12[:, T - 1, 1:2], a12[:, T - 1, 1:2], a_all[:, :], ALU.add))
            dve.tensor_reduce(a_max[:, :], a12[:, :, 1], AX_X, ALU.max).then_inc(s_am, 1)
            dve.wait_ge(s_am_t, 1)
            dve.tensor_reduce(a_max1[:, :], ps[0:1, 7, 0:P], AX_X, ALU.max).then_inc(s_am1, 1)
            dve.wait_ge(s_am_bc, 1)
            step(dve.tensor_copy(a_all[:, :], ps[:, 6, 0:1]))
            step(dve.tensor_scalar(csum[:, :], a12[:, :, 0], a_all[:, :], None, ALU.add))
            dve.tensor_scalar(cneg[:, :], csum[:, :], 0.0, None, ALU.min)
            dve.tensor_scalar(cpos[:, :], csum[:, :], 0.0, None, ALU.max)
            dve.tensor_scalar(agap[:, :], a12[:, :, 1], a_all[:, :], None, ALU.subtract).then_inc(s_cexp, 1)
            dve.wait_ge(s_pqfg, 1)
            for c in range(2):
                dve.tensor_tensor(diag[:, c * T:(c + 1) * T, :], ident.rearrange("p (o n) -> p o n", o=1).to_broadcast([P, T, P]),
                                  pq[:, c, :, None].to_broadcast([P, T, P]), ALU.mult).then_inc(s_diag, 1)
            for n in range(3):
                lo, hi = 4 * n * P, min(4 * n + 4, T) * P
                dve.wait_ge(s_pqr, 2 * n + 2)
                dve.tensor_copy(pq_rows[:, 1, lo:hi], ps[:, 2 * n + 1, 0:hi - lo]).then_inc(s_pq_dve, 1)
            dve.wait_ge(s_pq_dve, 3)

            def weigh(j, k, loaded):
                dve.wait_ge(s_t1, j + 1)
                dve.scalar_tensor_tensor(out=wgt[k][:, :], in0=pq_rows[:, 1, :], scalar=fg[:, 1, bass.ds(j, 1)],
                                         in1=wgt[k][:, :], op0=ALU.mult, op1=ALU.max).then_inc(s_t2, 1)
                dve.wait_ge(s_t2, j + 1)
                dve.wait_ge(s_adj1[k], loaded)
                dve.tensor_tensor(wgt_keep[:, bass.ds(j, 1), :].rearrange("p a n -> p (a n)"), wgt[k][:, GA * P:NP],
                                  adj1[k][:, GA * P:NP], ALU.mult)
                dve.tensor_tensor(wgt[k][:, 0:GA * P], wgt[k][:, 0:GA * P], adj1[k][:, 0:GA * P],
                                  ALU.mult).then_inc(s_w, 1)

            for j in range(2):
                weigh(j, j, 16)
            with dve.Fori(0, 3) as i:
                for k in range(3):
                    weigh(i * 3 + (2 + k), (2 + k) % 3, i * 16 + (16 if k == 0 else 32))

            def settle(n, banks, tiles):
                (b0, b1), (lo, hi) = banks, tiles
                step(dve.tensor_scalar(den[:, lo:hi], ps[:, b0:b1, D], 1.0e-9, None, ALU.add))
                step(dve.reciprocal(den[:, lo:hi], den[:, lo:hi]))
                for t in range(lo, hi):
                    dve.tensor_scalar(z[:, t, :], ps[:, b0 + t - lo, 0:D], den[:, t:t + 1], None,
                                      ALU.mult).then_inc(s_z, 1)

            def elu(n, lo, hi):
                dve.wait_ge(s_z, hi)
                zf = z[:, lo:hi, :].rearrange("p t d -> p (t d)")
                ef = hg_flat[:, lo * D:hi * D]
                xf = x_res[:, lo:hi, :].rearrange("p t d -> p (t d)")
                dve.tensor_scalar(ef, zf, 0.0, None, ALU.min).then_inc(s_elu, 1)
                dve.wait_ge(s_eexp, n + 1)
                step(dve.scalar_tensor_tensor(out=zf, in0=zf, scalar=0.0, in1=ef, op0=ALU.max, op1=ALU.add))
                step(dve.scalar_tensor_tensor(out=xf, in0=zf, scalar=-1.0, in1=xf, op0=ALU.add, op1=ALU.add))

            dve.wait_ge(s_g1, PRIMED + T)
            settle(0, (0, GA), (0, GA))
            dve.wait_ge(s_g1b, GB)
            settle(1, (0, GB), (GA, T))
            elu(0, 0, GA)
            elu(1, GA, T)

            norm(6, x_res, nat).then_inc(s_nat, 1)
            turned(3, None, None)
            choose(1)
            dve.wait_ge(s_pexp, 2)
            step(dve.tensor_reduce(psum_e[:, :], probs[:, :, :], AX_X, ALU.add))
            step(dve.reciprocal(psum_e[:, :], psum_e[:, :]))
            step(dve.tensor_tensor(probs[:, :, :], probs[:, :, :], over_e(psum_e), ALU.mult))
            step(dve.tensor_tensor(comb[:, :, :], probs[:, :, :], mask[:, :, :], ALU.mult))
            dve.wait_ge(s_pos, 2)
            step(dve.tensor_copy(cnt[:, :], ps[:, 0, 0:E]))
            full = cmp_eq[:, :, :, :].rearrange("p t j i -> p (t j i)")[:, 0:E * T].rearrange("p (e k) -> p e k", k=T)
            step(dve.tensor_tensor(full, cnt[:, :, None].to_broadcast([P, E, T]),
                                   const[:, C_K:C_K + T].rearrange("p (o k) -> p o k", o=1).to_broadcast([P, E, T]),
                                   ALU.is_gt))
            step(dve.tensor_reduce(tiles_e[:, :], full, AX_X, ALU.add))
            upto = cmp_eq[:, :, :, :].rearrange("p t j i -> p (t j i)")[:, 0:E * E].rearrange("p (e k) -> p e k", k=E)
            step(dve.tensor_tensor(upto, const[:, C_LE:C_LE + E * E].rearrange("p (e k) -> p e k", k=E),
                                   tiles_e[:, :].rearrange("p (o k) -> p o k", o=1).to_broadcast([P, E, E]), ALU.mult))
            step(dve.tensor_reduce(ends[:, :], upto, AX_X, ALU.add))
            step(dve.tensor_tensor(starts[:, :], ends[:, :], tiles_e[:, :], ALU.subtract))
            step(dve.tensor_scalar(starts[:, :], starts[:, :], float(P), 1.0, ALU.mult, ALU.add))
            step(dve.tensor_tensor(slot[:, :, :], pos, starts[:, :].rearrange("p (o e) -> p o e", o=1).to_broadcast([P, T, E]),
                                   ALU.add))
            step(dve.tensor_tensor(slot[:, :, :], slot[:, :, :], mask[:, :, :], ALU.mult))
            step(dve.tensor_reduce(sa[:, :], slot[:, :, :], AX_X, ALU.max))
            step(dve.tensor_reduce(sb_[:, :], slot[:, :, :], AX_X, ALU.add))
            step(dve.tensor_tensor(sb_[:, :], sb_[:, :], sa[:, :], ALU.subtract))
            row_number(sa, 0)
            dve.wait_ge(s_idx, 2)
            row_number(sb_, 1)
            step(dve.tensor_tensor(mask[:, :, :], slot[:, :, :], over_e(sa), ALU.is_equal))
            step(dve.tensor_tensor(mask[:, :, :], mask[:, :, :], comb[:, :, :], ALU.mult))
            dve.tensor_reduce(ca[:, :], mask[:, :, :], AX_X, ALU.add)
            step(dve.tensor_reduce(cb[:, :], comb[:, :, :], AX_X, ALU.add))
            step(dve.tensor_tensor(cb[:, :], cb[:, :], ca[:, :], ALU.subtract))
            which = cmp_gt[:, :, :, :].rearrange("p t j i -> p (t j i)")[:, 0:E * (TILES1 + 1)].rearrange("p (k e) -> p k e", e=E)
            step(dve.tensor_tensor(which, const[:, C_TILE:C_TILE + TILES1 + 1, None].to_broadcast([P, TILES1 + 1, E]),
                                   ends[:, :].rearrange("p (o e) -> p o e", o=1).to_broadcast([P, TILES1 + 1, E]),
                                   ALU.is_ge))
            step(dve.tensor_reduce(texp[:, :], which, AX_X, ALU.add))
            dve.tensor_scalar(tile_expert[:, :], texp[:, :], float(E - 1), None, ALU.min).then_inc(s_te, 1)
            dve.wait_ge(s_combt_ps, 1)
            for n in range(3):
                lo, hi = 4 * n * P, min(4 * n + 4, T) * P
                last = dve.tensor_copy(comb_t[:, lo:hi], ps[0:E, n, 0:hi - lo])
            last.then_inc(s_combt, 1)
            for t in range(T):
                dve.wait_ge(s_b2, t + 1)
                dve.tensor_tensor(x_res[:, t, :], x_res[:, t, :], ps[:, 2 + t % 6, 0:D], ALU.add).then_inc(s_b2_add, 1)

            def x1_copy(t):
                dve.wait_ge(s_x1_ps, t + 1)
                dve.wait_ge(s_h1_ps, t)
                dve.tensor_copy(x1t_t[:, :, :], ps[:, 0, 0:DT * P].rearrange("p (c n) -> p c n", n=P)).then_inc(s_x1t, 1)

            def h1_copy(t):
                dve.wait_ge(s_h1_ps, t + 1)
                dve.wait_ge(s_h1t_ps, t)
                dve.tensor_copy(h1pre[:, :].rearrange("p (b n) -> p b n", b=2), ps[:, 2:4, :]).then_inc(s_h1pre, 1)

            def y1_copy(t):
                dve.wait_ge(s_y1_ps, PRIMED + t + 1)
                dve.wait_ge(s_y1o, PRIMED + t * 16)
                dve.tensor_copy(y1t[:, :], ps[:, 6, 0:D]).then_inc(s_y1, 1)

            x1_copy(0)
            h1_copy(0)
            x1_copy(1)
            with dve.Fori(0, TILES1 - 2) as t:
                h1_copy(t + 1)
                y1_copy(t)
                x1_copy(t + 2)
            h1_copy(TILES1 - 1)
            y1_copy(TILES1 - 2)
            y1_copy(TILES1 - 1)
            dve.wait_ge(s_gath1, 2 * 16 * T)
            dve.wait_ge(s_b2_add, T)
            for t in range(T):
                last = dve.scalar_tensor_tensor(out=x_res[:, t, :], in0=nat[:, t, :], scalar=ca[:, t:t + 1],
                                                in1=x_res[:, t, :], op0=ALU.mult, op1=ALU.add)
            step(last)
            for t in range(T):
                last = dve.scalar_tensor_tensor(out=x_res[:, t, :], in0=u[:, t, :], scalar=cb[:, t:t + 1],
                                                in1=x_res[:, t, :], op0=ALU.mult, op1=ALU.add)
            last.then_inc(s_fin, 1)


def _tiles(w):
    return w.reshape(-1, P, w.shape[-1]).transpose(1, 0, 2)


def _columns(v):
    return v.reshape(-1, P).T


def _experts(w1, b1, w2, b2):
    one = [np.concatenate([_tiles(w1[e]).reshape(P, -1), _tiles(w2[e]).reshape(P, -1), _columns(b1[e])]
                          + ([_columns(b2[e])] if b2 is not None else []), axis=1) for e in range(E)]
    return np.stack(one)


def kernel(**inputs):
    import concourse.bacc as _bacc
    from concourse.bass_utils import run_bass_kernel_spmd as _run

    i = {k: np.asarray(v) for k, v in inputs.items()}
    x = np.zeros((NP, D), np.float32)
    x[:N] = i["x"]
    adj_t = np.zeros((NP, NP), np.float32)
    adj_t[:N, :N] = i["adj"].T
    vecs = np.zeros((P, V_END), np.float32)
    for at, name in ((V_G1, "ln1_g"), (V_B1, "ln1_b"), (V_G2, "ln2_g"), (V_B2, "ln2_b"), (V_BQ, "bq"), (V_BK, "bk")):
        vecs[:, at:at + DT] = _columns(i["L0_ffn_" + name])
    vecs[0:E, V_RB] = i["L0_ffn_router_b"]
    vecs[0:E, V_GB] = i["L1_ffn_bg"]
    arrays = {
        "x": x,
        "adj_t": adj_t,
        "const": shape_constants(),
        "rows": np.concatenate([i["L0_ffn_bv"], i["L0_ffn_bo"], i["L0_gnn_W"]]),
        "vecs": vecs,
        "w_attn": np.stack([_tiles(i["L0_ffn_" + n]) for n in ("wq", "wk", "wv", "wo")], axis=1),
        "w_graph": _tiles(i["L1_gnn_W"]),
        "w_graph_t": _tiles(i["L1_gnn_W"].T),
        "attn_lr": _tiles(np.concatenate([i["L1_gnn_attn_l"], i["L1_gnn_attn_r"]], axis=1)),
        "w_router": np.stack([_tiles(i["L0_ffn_router_w"]), _tiles(i["L1_ffn_Wg"])], axis=1),
        "b2_l1": i["L1_ffn_b2"],
        "w_l0": _experts(i["L0_ffn_w1"], i["L0_ffn_b1"], i["L0_ffn_w2"], i["L0_ffn_b2"]),
        "w_l1": _experts(i["L1_ffn_W1"], i["L1_ffn_b1"], i["L1_ffn_W2"], None).transpose(1, 0, 2),
    }
    arrays = {k: np.ascontiguousarray(v) for k, v in arrays.items()}
    nc = _bacc.Bacc("TRN2", target_bir_lowering=False, num_devices=1)
    aps = {k: nc.dram_tensor(k, v.shape, mybir.dt.from_np(v.dtype), kind="ExternalInput").ap() for k, v in arrays.items()}
    out = nc.dram_tensor("out", (N, D), F32, kind="ExternalOutput").ap()
    build_program(nc, aps, out)
    return _run(nc, [arrays], core_ids=[0]).results[0]["out"]
```

```python
from contextlib import ExitStack

import numpy as np

import concourse.bass as bass
from concourse import mybir

F32 = mybir.dt.float32
F32R = mybir.dt.float32r
BF16 = mybir.dt.bfloat16
I32 = mybir.dt.int32
ALU = mybir.AluOpType
ACT = mybir.ActivationFunctionType
AX_X = mybir.AxisListType.X

P = 128
N = 1354
D = 256
DT = D // P
T = -(-N // P)
NP = T * P
LAST = N - (T - 1) * P
H = 8
DK = D // H
QC = 340
QB = 4
HALF = 2 * QC
NC4 = NP // QB
E = 8
F = 1024
FT = F // P
CAP = int(np.ceil(N * 1.6 / E))
CAPP = CAP + CAP % 2
CT = -(-CAPP // P)
CREM = CAPP - (CT - 1) * P
SLOTS0 = E * CAPP
TILES1 = (2 * N + E * (P - 1)) // P
SLOTS1 = TILES1 * P
WCOLS = DT * F + FT * D + FT + DT
B1AT = DT * F + FT * D
B2AT = B1AT + FT
W1COLS = B2AT
FAR = 1.0e6
UNDER = -87.3365
EPS = 1e-5
SCALE = float(1.0 / np.sqrt(np.float32(DK)))
GA = 8
GB = T - GA
X_PARTS = ((0, 4), (4, 8), (8, T))

C_ID = 0
C_TRI = C_ID + P
C_VALID = C_TRI + P
C_LT = C_VALID + T
C_OFF = C_LT + E * E
C_LE = C_OFF + E
C_K = C_LE + E * E
C_TILE = C_K + T
C_END = C_TILE + TILES1 + 1

V_G1, V_B1, V_G2, V_B2, V_BQ, V_BK = (2 * i for i in range(6))
V_RB, V_GB = 12, 13
V_END = 14


def shape_constants():
    c = np.zeros((P, C_END), np.float32)
    c[:, C_ID:C_ID + P] = np.eye(P)
    c[:, C_TRI:C_TRI + P] = np.triu(np.ones((P, P)), 1)
    tok = np.arange(T)[None, :] * P + np.arange(P)[:, None]
    c[:, C_VALID:C_VALID + T] = tok < N
    j, i = np.meshgrid(np.arange(E), np.arange(E), indexing="ij")
    c[:, C_LT:C_LT + E * E] = (j < i).reshape(1, -1)
    c[:, C_OFF:C_OFF + E] = np.arange(E) * CAPP + 1
    c[:, C_LE:C_LE + E * E] = (i <= j).reshape(1, -1)
    c[:, C_K:C_K + T] = np.arange(T) * P
    c[:, C_TILE:C_TILE + TILES1 + 1] = np.arange(TILES1 + 1)
    return c


def build_program(nc, a, out):
    with ExitStack() as ctx:
        base = -(-nc.sbuf_base // 32) * 32
        top = nc.sbuf_top
        cursor = [base]

        offsets = {}

        def place(name, shape, dtype=F32, parts=P):
            offsets[name] = cursor[0]
            size = int(np.prod(shape)) * (2 if dtype == BF16 else 4)
            t = nc.alloc_sbuf_tensor_at(name, [parts] + list(shape), dtype, offset=cursor[0])
            cursor[0] += -(-size // 32) * 32
            assert cursor[0] <= top, (name, cursor[0], top)
            return t

        x_res = place("x_res", [T, D])
        u_or_h = place("u_or_h", [T * (D + 2)])
        u = u_or_h[:, 0:T * D].rearrange("p (t d) -> p t d", t=T)
        hg = u_or_h[:, :].rearrange("p (t d) -> p t d", t=T)
        nat = place("nat", [T, D])
        nt = place("nt", [DT, NP])
        const = place("const", [C_END])
        ones = place("ones", [P])
        tri_b = place("tri_b", [P], BF16)
        ones_b = place("ones_b", [P], BF16)
        vecs = place("vecs", [V_END])
        rows = place("rows", [3, D])
        w_attn = place("w_attn", [4, DT, D])
        w_graph = place("w_graph", [DT, D + 2])
        w_graph_t = place("w_graph_t", [DT, D])
        attn_lr = place("attn_lr", [DT, 2])
        w_router = place("w_router", [2, DT, E])
        b2_l1 = place("b2_l1", [D], F32, E)
        stats = place("stats", [T, 6])
        mv = place("mv", [T, 2])
        var = place("var", [T])
        std = place("std", [T])
        rstd = place("rstd", [T])
        shift = place("shift", [T])
        rstd_u = place("rstd_u", [T])
        shift_u = place("shift_u", [T])
        lgt = place("lgt", [NP], F32, E)
        lg = place("lg", [T, E])
        top1 = place("top1", [T])
        probs = place("probs", [T, E])
        psum_e = place("psum_e", [T])
        cmp_gt = place("cmp_gt", [T, E, E])
        cmp_eq = place("cmp_eq", [T, E, E])
        mask = place("mask", [T, E])
        mask_b = place("mask_b", [T, E], BF16)
        slot = place("slot", [T, E])
        sa = place("sa", [T])
        sb_ = place("sb_", [T])
        skip = place("skip", [T])
        idx = place("idx", [2, T], I32)
        comb = place("comb", [T, E])
        ca = place("ca", [T])
        cb = place("cb", [T])
        cnt = place("cnt", [E])
        tiles_e = place("tiles_e", [E])
        ends = place("ends", [E])
        starts = place("starts", [E])
        texp = place("texp", [TILES1 + 1])
        tile_expert = place("tile_expert", [TILES1 + 1], I32)
        zeros = place("zeros", [D])
        arena = cursor[0]
        assert arena + E * W1COLS * 4 <= top, (arena, top)

        w_l1 = place("w_l1", [E, W1COLS])
        half_l1 = arena + 4 * W1COLS * 4
        cursor[0] = arena
        adj0 = [place(f"adj0_{i}", [NP]) for i in range(3)]
        cursor[0] = arena
        w_l0 = [place(f"w_l0_{i}", [WCOLS]) for i in range(2)]
        attn_at = cursor[0]
        v_hi = place("v_hi", [T, D], F32R)
        v_lo = place("v_lo", [T, D], F32R)
        v_st = [place(f"v_st{i}", [T, 3 * DK], F32R) for i in range(2)]
        q_st = [place(f"q_st{i}", [NP], F32R) for i in range(2)]
        k_st = [place(f"k_st{i}", [NP], F32R) for i in range(2)]
        expo = [place(f"expo{i}", [HALF]) for i in range(4)]
        expo_hi = [place(f"expo_hi{i}", [HALF], F32R) for i in range(4)]
        expo_lo = [place(f"expo_lo{i}", [HALF], F32R) for i in range(4)]
        ctx_raw = [place(f"ctx_raw{i}", [HALF], F32, 3 * DK) for i in range(2)]
        den_all = place("den_all", [P], F32, H * T)
        mx4 = place("mx4", [T, QB])
        negm = place("negm", [T])
        m_hl = place("m_hl", [2 * T], F32R)
        m_rows = place("m_rows", [P], F32R, 2 * T)
        cursor[0] = offsets["expo0"]
        proj = [place(f"proj{i}", [NC4]) for i in range(2)]
        proj_hi = [place(f"proj_hi{i}", [NC4], F32R) for i in range(2)]
        proj_lo = [place(f"proj_lo{i}", [NC4], F32R) for i in range(2)]
        v_tmp = [place(f"v_tmp{i}", [D]) for i in range(2)]
        assert cursor[0] <= offsets["expo_lo0"]
        cursor[0] = attn_at
        den_rows = place("den_rows", [DT, NP])
        ctx_low = place("ctx_low", [DT, NP])
        assert cursor[0] <= offsets["expo0"]
        cursor[0] = attn_at
        xs0 = [place(f"xs0_{i}", [CT, D]) for i in range(2)]
        xs0_t = place("xs0_t", [DT, CAPP])
        h0 = place("h0", [FT, CAPP])
        y0_t = place("y0_t", [DT, CAPP])
        y0 = [place(f"y0_{i}", [CT, D]) for i in range(2)]
        assert cursor[0] <= half_l1
        cursor[0] = arena
        adj1 = [place(f"adj1_{i}", [NP]) for i in range(3)]
        wgt = [place(f"wgt{i}", [NP]) for i in range(3)]
        wgt_keep = place("wgt_keep", [T, GB * P])
        a12 = place("a12", [T, 2])
        a_max = place("a_max", [1])
        a_maxr = place("a_maxr", [P], F32, 1)
        a_max1 = place("a_max1", [1], F32, 1)
        a_all = place("a_all", [1])
        csum = place("csum", [T])
        cneg = place("cneg", [T])
        cpos = place("cpos", [T])
        agap = place("agap", [T])
        pq = place("pq", [2, T])
        fg = place("fg", [2, T])
        den = place("den", [T])
        assert cursor[0] <= half_l1
        cursor[0] = offsets["wgt0"]
        elu_exp = place("elu_exp", [GA * D])
        assert cursor[0] <= offsets["wgt_keep"]
        ident = const[:, C_ID:C_ID + P]
        valid = const[:, C_VALID:C_VALID + T]
        diag = nat[:, :, :].rearrange("p t d -> p (t d)").rearrange("p (k c) -> p k c", c=P)
        pq_rows = nt
        z = nat
        cursor[0] = offsets["w_attn"]
        x1t = place("x1t", [D])
        x1t_t = place("x1t_t", [DT, P])
        y1t = place("y1t", [D])
        assert cursor[0] <= offsets["w_graph"]
        cursor[0] = offsets["nt"]
        h1pre = place("h1pre", [F])
        h1 = place("h1", [FT, P])
        assert cursor[0] <= offsets["const"]
        comb_t = lgt

        ps = ctx.enter_context(nc.psum_tensor("ps", [P, 8, 512], F32))

        def normed_dve(k, t=T - 1):
            return (k - 1) * ((T + 1) // 2) + t // 2 + 1

        def normed_act(k, t=T - 1):
            return (k - 1) * (T // 2) + (t + 1) // 2

        def scratch(name, shape):
            return nc.dram_tensor(name, shape, F32, kind="Internal").ap()

        q_hi_d, q_lo_d, k_hi_d, k_lo_d = (scratch(n, [D, NP]) for n in ("q_hi_d", "q_lo_d", "k_hi_d", "k_lo_d"))
        ctx_hi_d, ctx_lo_d = scratch("ctx_hi_d", [D, NP]), scratch("ctx_lo_d", [D, NP])
        den_d, inv_d = scratch("den_d", [H, NP]), scratch("inv_d", [H, NP])
        xs0_d, ys0_d = scratch("xs0_d", [SLOTS0, D]), scratch("ys0_d", [SLOTS0, D])
        xs1_d, ys1_d = scratch("xs1_d", [SLOTS1, D]), scratch("ys1_d", [SLOTS1, D])

        def sem(name):
            return ctx.enter_context(nc.semaphore(name))

        s_x = [sem(f"x_loaded{n}") for n in range(len(X_PARTS))]
        s_x1 = sem("graph0_added")
        s_const = sem("const_loaded")
        s_wts = sem("small_weights_loaded")
        s_adj0 = [sem(f"adj0_loaded{i}") for i in range(3)]
        s_ones = sem("ones_ready")
        s_step = sem("dve_step")
        s_var = sem("variance_ready")
        s_std = sem("std_ready")
        s_norm_dve = sem("normed_by_dve")
        s_norm_act = sem("normed_by_act")
        s_rstd = sem("inverse_std_ready")
        s_u1 = sem("block_input_ready")
        s_x1u = sem("two_residuals_added")
        s_hid = sem("hidden_ready")
        s_g0_row = sem("graph0_row_done")
        s_x1 = sem("x1_ready")
        s_tr = sem("transposes_done")
        s_tr_act = sem("transposed_by_act")
        s_tr_dve = sem("transposed_by_dve")
        s_qk_ps = sem("qk_product_done")
        s_qk_raw = sem("qk_biased")
        s_qk_hi = sem("qk_high_ready")
        s_qk_lo = sem("qk_low_ready")
        s_qk_out = [sem(f"qk_written{i}") for i in range(2)]
        s_v_ps = sem("v_product_done")
        s_vz = sem("v_pad_zeroed")
        s_v = sem("v_ready")
        s_v_st = [sem(f"v_stack_loaded{i}") for i in range(2)]
        s_stack = [sem(f"qk_stack_loaded{i}") for i in range(2)]
        s_kone = sem("k_ones_ready")
        s_s1 = sem("scores_for_max_done")
        s_mx = sem("chunk_max_ready")
        s_mq = sem("max_stats_step")
        s_hl = sem("neg_max_ready")
        s_mt = sem("neg_max_transposed")
        s_mrow = sem("neg_max_rows_ready")
        s_mload = [sem(f"neg_max_loaded{i}") for i in range(2)]
        s_s2 = sem("scores_done")
        s_exp = sem("exp_ready")
        s_av = sem("attn_product_done")
        s_lo = [sem("exp_low_by_pool"), sem("exp_low_by_dve")]
        s_cr = sem("ctx_copied")
        s_cout = [sem(f"ctx_half_written{i}") for i in range(2)]
        s_cpad = sem("ctx_pad_written")
        s_den = sem("denominators_loaded")
        s_inv = sem("inverse_ready")
        s_invd = sem("inverse_written")
        s_cin = sem("ctx_loaded")
        s_inv_in = sem("inverse_denominators_loaded")
        s_ctx = sem("ctx_normed")
        s_vt = sem("v_biased")
        s_vhi = sem("v_high_ready")
        s_wo = sem("out_product_done")
        s_u2 = sem("u2_ready")
        s_lgt_ps = sem("router_product_done")
        s_lgt = sem("router_rows_ready")
        s_lg_ps = sem("router_transposed")
        s_lg = sem("logits_ready")
        s_pexp = sem("router_exp_ready")
        s_mask = sem("mask_ready")
        s_pos = sem("positions_done")
        s_idx = sem("row_numbers_ready")
        s_zero = sem("zeros_ready")
        s_zfill = sem("scratch_zeroed")
        s_scat = sem("rows_scattered")
        s_xs0 = [sem(f"xs0_loaded{i}") for i in range(2)]
        s_w0 = [sem(f"w_l0_loaded{i}") for i in range(2)]
        s_xt_ps = sem("xs0_transposed")
        s_xt = sem("xs0_t_ready")
        s_h0_ps = sem("h0_product_done")
        s_h0 = sem("h0_ready")
        s_y0_ps = sem("y0_product_done")
        s_yt = sem("y0_t_ready")
        s_yo_ps = sem("y0_transposed")
        s_yo = sem("y0_ready")
        s_ys = [sem(f"ys0_written{i}") for i in range(2)]
        s_gz = sem("gather_zeroed")
        s_gath = [sem(f"rows_gathered{t}") for t in range(T)]
        s_x2 = sem("x2_ready")
        s_wal = sem("attn_weight_product_done")
        s_wal_sb = sem("attn_weight_ready")
        s_hg_ps = sem("graph_features_done")
        s_hg = sem("graph_features_ready")
        s_am = sem("max_column_ready")
        s_am_t = sem("max_column_transposed")
        s_am1 = sem("max_ready")
        s_am_bc = sem("max_broadcast")
        s_cexp = sem("factor_logs_ready")
        s_pqfg = sem("factors_ready")
        s_diag = sem("diagonals_ready")
        s_pqr = sem("factor_rows_done")
        s_pq_act = sem("factor_rows_by_act")
        s_pq_dve = sem("factor_rows_by_dve")
        s_adj1 = [sem(f"adj1_loaded{i}") for i in range(3)]
        s_t1 = sem("positive_branch_ready")
        s_t2 = sem("branches_maxed")
        s_w = sem("graph_weights_ready")
        s_g1 = sem("graph1_row_done")
        s_g1b = sem("graph1_rest_done")
        s_z = sem("graph1_normed")
        s_elu = sem("elu_min_ready")
        s_eexp = sem("elu_exp_ready")
        s_w1 = sem("w_l1_loaded")
        s_scat1 = sem("rows_scattered1")
        s_te = sem("tile_experts_ready")
        s_x1l = sem("xs1_loaded")
        s_x1_ps = sem("xs1_transposed")
        s_x1t = sem("xs1_t_ready")
        s_h1_ps = sem("h1_product_done")
        s_h1pre = sem("h1_copied")
        s_h1t_ps = sem("h1_transposed")
        s_h1 = sem("h1_ready")
        s_y1_ps = sem("y1_product_done")
        s_y1 = sem("y1_ready")
        s_y1o = sem("ys1_written")
        s_combt_ps = sem("comb_transposed")
        s_combt = sem("comb_t_ready")
        s_b2 = sem("b2_products_done")
        s_x2 = sem("layer0_tile_summed")
        s_first = sem("first_expert_added")
        s_fin = sem("output_tile_ready")
        s_out = sem("output_written")

        s_b2_add = sem("b2_added")

        qk_chunks = [(hi_d, lo_d, mt, c) for hi_d, lo_d in ((q_hi_d, q_lo_d), (k_hi_d, k_lo_d))
                     for mt in range(DT) for c in range(QB)]
        w_l0_b2 = [w[:, B2AT:B2AT + DT] for w in w_l0]
        hg_flat = u_or_h[:, 0:T * D]
        UNITS = 2 * T
        CHUNKS = T * QB
        WTS = 16 * 7

        PRIMED = 1
        primed = [s_exp, *s_lo, s_av, s_cr, *s_cout, s_h0, s_y0_ps, s_yt, s_yo_ps, s_yo, *s_ys,
                  s_g1, s_y1_ps, s_y1, s_y1o]

        block = ctx.enter_context(nc.Block())

        beside = {m: 3 if m % 2 else 2 for m in range(17)} | {17: 2}
        MT_AT = 18
        assert sum(beside.values()) == T * QB
        LAG = 1
        by_dve = [m in (6, 12, 19, 21) for m in range(UNITS)]

        def low_count(g):
            k, m = divmod(g, UNITS)
            return by_dve[m], k * by_dve.count(by_dve[m]) + by_dve[:m + 1].count(by_dve[m])

        def lows_taken(i, who):
            return i * (2 * by_dve.count(who))

        def take_low(engine, i, g):
            before = i * (2 * UNITS) + g
            engine.wait_ge(s_exp, PRIMED + before + 1)
            engine.wait_ge(s_av, PRIMED + (before - 3 if g > 2 else i * (2 * UNITS)))
            engine.tensor_tensor(expo_lo[g % 4][:, :], expo[g % 4][:, :], expo_hi[g % 4].bitcast(F32)[:, :],
                                 ALU.subtract).then_inc(s_lo[low_count(g)[0]], 1)


        @block.sync
        def _(sp):
            for n, (lo, hi) in enumerate(X_PARTS):
                sp.dma_start(x_res[:, lo:hi, :], a["x"][lo * P:hi * P, :].rearrange("(t p) d -> p t d", p=P)).then_inc(s_x[n], 16)
            sp.dma_start(const[:, :], a["const"]).then_inc(s_const, 16)
            sp.dma_start(rows[:, :, :].rearrange("p a d -> p (a d)"),
                         a["rows"].partition_broadcast(P)).then_inc(s_const, 16)
            adj = a["adj_t"].rearrange("(t p) n -> t p n", p=P)
            for j in range(3):
                sp.dma_start(adj0[j][:, :], adj[j]).then_inc(s_adj0[j], 16)
            for name, dst in (("vecs", vecs[:, :]), ("w_attn", w_attn[:, :, :, :]), ("w_graph", w_graph[:, :, 0:D]),
                              ("w_graph_t", w_graph_t[:, :, :]), ("attn_lr", attn_lr[:, :, :]),
                              ("w_router", w_router[:, :, :, :]), ("b2_l1", b2_l1[:, :])):
                sp.dma_start(dst, a[name]).then_inc(s_wts, 16)
            def load_row(slots, loaded, readers, j, k):
                sp.wait_ge(readers, j - 2)
                sp.dma_start(slots[k][:, :], adj[j]).then_inc(loaded[k], 16)

            with sp.Fori(0, (T - 3) // 3) as i:
                for k in range(3):
                    load_row(adj0, s_adj0, s_g0_row, i * 3 + (3 + k), k)
            for j in range(3 + (T - 3) // 3 * 3, T):
                load_row(adj0, s_adj0, s_g0_row, j, j % 3)
            sp.wait_ge(s_zero, 1)
            sp.dma_start(xs0_d.rearrange("(k p) d -> p k d", p=P),
                         zeros[:, None, :].to_broadcast([P, SLOTS0 // P, D])).then_inc(s_zfill, 16)
            sp.dma_start(xs1_d.rearrange("(k p) d -> p k d", p=P),
                         zeros[:, None, :].to_broadcast([P, TILES1, D])).then_inc(s_zfill, 16)
            sp.wait_ge(s_g0_row, T)
            for e in range(2):
                sp.dma_start(w_l0[e][:, :], a["w_l0"][e]).then_inc(s_w0[e], 16)
            for n, (hi_d, lo_d, mt, c) in enumerate(qk_chunks):
                there = (slice(mt * P, mt * P + P), slice(c * NC4, c * NC4 + NC4))
                sp.wait_ge(s_qk_hi, n + 1)
                sp.dma_start(hi_d[there], proj_hi[n % 2].bitcast(F32)[:, :]).then_inc(s_qk_out[n % 2], 16)
                sp.wait_ge(s_qk_lo, n + 1)
                sp.dma_start(lo_d[there], proj_lo[n % 2].bitcast(F32)[:, :]).then_inc(s_qk_out[n % 2], 16)
            for k in range(2):
                sp.wait_ge(s_qk_out[k], 16 * len(qk_chunks))

            def load_stack(k, h):
                for b, src in enumerate((q_hi_d, q_hi_d, q_lo_d)):
                    sp.dma_start(q_st[k].bitcast(F32)[b * DK:(b + 1) * DK, :],
                                 src[bass.ds(h * DK, DK), :]).then_inc(s_stack[k], 16)
                for b, src in enumerate((k_hi_d, k_lo_d, k_hi_d)):
                    sp.dma_start(k_st[k].bitcast(F32)[b * DK:(b + 1) * DK, :],
                                 src[bass.ds(h * DK, DK), :]).then_inc(s_stack[k], 16)

            def load_values(k, h):
                for b, src in enumerate((v_hi, v_lo)):
                    sp.dma_start(v_st[k].bitcast(F32)[:, :, b * DK:(b + 1) * DK],
                                 src.bitcast(F32)[:, :, bass.ds(h * DK, DK)]).then_inc(s_v_st[k], 16)

            def load_max(k, h):
                sp.wait_ge(s_mrow, h + 1)
                sp.dma_start(q_st[k].bitcast(F32)[3 * DK:3 * DK + 2, :].rearrange("c (t p) -> c t p", p=P),
                             m_rows.bitcast(F32)[:, :]).then_inc(s_mload[k], 16)

            load_stack(0, 0)
            load_stack(1, 1)
            sp.wait_ge(s_v, T)
            load_values(0, 0)
            load_values(1, 1)
            load_max(0, 0)
            for part_d in (ctx_hi_d, ctx_lo_d):
                sp.dma_start(part_d[:, 2 * HALF:NP].rearrange("(c p) n -> p c n", p=P),
                             zeros[:, 0:DT * (NP - 2 * HALF)].rearrange("p (c n) -> p c n", c=DT)).then_inc(s_cpad, 16)
            sp.dma_start(den_d[:, 2 * HALF:NP], ones[0:H, 0:NP - 2 * HALF]).then_inc(s_cpad, 16)

            def store_half(h, half):
                sp.wait_ge(s_cr, PRIMED + h * 2 + (half + 1))
                cols = slice(half * HALF, (half + 1) * HALF)
                sp.dma_start(den_d[bass.ds(h, 1), cols], ctx_raw[half][2 * DK:2 * DK + 1, :]).then_inc(s_cout[half], 16)
                for b, part_d in enumerate((ctx_hi_d, ctx_lo_d)):
                    sp.dma_start(part_d[bass.ds(h * DK, DK), cols],
                                 ctx_raw[half][b * DK:(b + 1) * DK, :]).then_inc(s_cout[half], 16)

            def heads(i, last):
                for k in range(2):
                    h = i * 2 + k
                    store_half(h, 0)
                    if not (last and k):
                        load_max(1 - k, h + 1)
                    if not last:
                        sp.wait_ge(s_s2, h * UNITS + UNITS)
                        load_stack(k, h + 2)
                    store_half(h, 1)
                    if not last:
                        load_values(k, h + 2)

            with sp.Fori(0, H // 2 - 1) as i:
                heads(i, False)
            heads(H // 2 - 1, True)
            for half in range(2):
                sp.wait_ge(s_cout[half], PRIMED + 48 * H)
            sp.wait_ge(s_cpad, 48)
            sp.dma_start(den_all[:, :], den_d.rearrange("h (t p) -> (h t) p", p=P)).then_inc(s_den, 16)
            sp.dma_start(nt[:, :, :], ctx_hi_d.rearrange("(c p) n -> p c n", p=P)).then_inc(s_cin, 16)
            sp.dma_start(ctx_low[:, :, :], ctx_lo_d.rearrange("(c p) n -> p c n", p=P)).then_inc(s_cin, 16)
            sp.wait_ge(s_inv, 1)
            sp.dma_start(inv_d.rearrange("h (t p) -> (h t) p", p=P), den_all[:, :]).then_inc(s_invd, 16)
            sp.wait_ge(s_invd, 16)
            for c in range(DT):
                sp.dma_start(den_rows[:, c, :], inv_d[c * (H // DT):(c + 1) * (H // DT), None, :]
                             .to_broadcast([H // DT, DK, NP])).then_inc(s_inv_in, 16)
            sp.wait_ge(s_ctx, 1)
            sp.dma_start(w_l1[:, E // 2:E, :], a["w_l1"][:, E // 2:E, :]).then_inc(s_w1, 16)

            def load_xs0(k, e):
                sp.dma_start(xs0[k][:, 0:CT - 1, :], xs0_d[bass.ds(e * CAPP, (CT - 1) * P), :]
                             .rearrange("(c p) d -> p c d", p=P)).then_inc(s_xs0[k], 16)
                sp.dma_start(xs0[k][0:CREM, CT - 1, :],
                             xs0_d[bass.ds(e * CAPP + (CT - 1) * P, CREM), :]).then_inc(s_xs0[k], 16)

            sp.wait_ge(s_scat, 16 * T)
            load_xs0(0, 0)
            load_xs0(1, 1)

            def experts(i, last):
                for k in range(2):
                    e = i * 2 + k
                    if not last:
                        sp.wait_ge(s_yt, PRIMED + e + 1)
                        sp.dma_start(w_l0[k][:, :], a["w_l0"][bass.ds(e + 2, 1), :, :]
                                     .rearrange("a p n -> p (a n)")).then_inc(s_w0[k], 16)
                        load_xs0(k, e + 2)
                    sp.wait_ge(s_yo, PRIMED + e + 1)
                    sp.dma_start(ys0_d[bass.ds(e * CAPP, (CT - 1) * P), :].rearrange("(c p) d -> p c d", p=P),
                                 y0[k][:, 0:CT - 1, :]).then_inc(s_ys[k], 16)
                    sp.dma_start(ys0_d[bass.ds(e * CAPP + (CT - 1) * P, CREM), :],
                                 y0[k][0:CREM, CT - 1, :]).then_inc(s_ys[k], 16)

            with sp.Fori(0, E // 2 - 1) as i:
                experts(i, False)
            experts(E // 2 - 1, True)

            sp.wait_ge(s_y0_ps, PRIMED + E)
            for j in range(3):
                sp.dma_start(adj1[j][:, :], adj[j]).then_inc(s_adj1[j], 16)
            with sp.Fori(0, (T - 3) // 3) as i:
                for k in range(3):
                    load_row(adj1, s_adj1, s_w, i * 3 + (3 + k), k)
            for j in range(3 + (T - 3) // 3 * 3, T):
                load_row(adj1, s_adj1, s_w, j, j % 3)
            sp.wait_ge(s_z, T)
            sp.dma_start(w_l1[:, 0:E // 2, :], a["w_l1"][:, 0:E // 2, :]).then_inc(s_w1, 16)

            sp.wait_ge(s_scat1, 2 * 16 * T)
            sp.dma_start(x1t[:, :], xs1_d[0:P, :]).then_inc(s_x1l, 16)
            sp.wait_ge(s_x1_ps, 1)
            sp.dma_start(x1t[:, :], xs1_d[P:2 * P, :]).then_inc(s_x1l, 16)
            sp.wait_ge(s_x1_ps, 2)
            sp.dma_start(x1t[:, :], xs1_d[2 * P:3 * P, :]).then_inc(s_x1l, 16)

            def store_y1(t):
                sp.wait_ge(s_y1, PRIMED + t + 1)
                sp.dma_start(ys1_d[bass.ds(t * P, P), :], y1t[:, :]).then_inc(s_y1o, 16)

            with sp.Fori(0, TILES1 - 3) as t:
                store_y1(t)
                sp.wait_ge(s_x1_ps, t + 3)
                sp.dma_start(x1t[:, :], xs1_d[bass.ds(t * P + 3 * P, P), :]).then_inc(s_x1l, 16)
            for t in range(TILES1 - 3, TILES1):
                store_y1(t)
            for lo, hi in ((0, 5), (5, 9), (9, T - 1)):
                sp.wait_ge(s_fin, hi)
                sp.dma_start(out[lo * P:hi * P, :].rearrange("(t p) d -> p t d", p=P),
                             x_res[:, lo:hi, :]).then_inc(s_out, 16)
            sp.wait_ge(s_fin, T)
            sp.dma_start(out[(T - 1) * P:N, :], x_res[0:LAST, T - 1, :]).then_inc(s_out, 16)
            sp.wait_ge(s_out, 4 * 16)

        @block.gpsimd
        def _(pool):
            for s in primed:
                pool.sem_inc(s, PRIMED)
            pool.memset(zeros[:, :], 0.0).then_inc(s_zero, 1)
            pool.memset(ones[:, :], 1.0).then_inc(s_ones, 1)
            for v in (v_hi, v_lo):
                pool.memset(v.bitcast(F32)[:, T - 1, :], 0.0).then_inc(s_vz, 1)
            for k in range(2):
                pool.memset(v_st[k].bitcast(F32)[:, 0:T - 1, 2 * DK:3 * DK], 1.0).then_inc(s_vz, 1)
                pool.memset(v_st[k].bitcast(F32)[:, T - 1, 2 * DK:3 * DK], 0.0).then_inc(s_vz, 1)
            pool.wait_ge(s_vz, 6)
            for k in range(2):
                pool.memset(v_st[k].bitcast(F32)[0:LAST, T - 1, 2 * DK:3 * DK], 1.0).then_inc(s_vz, 1)
                pool.memset(k_st[k].bitcast(F32)[3 * DK:3 * DK + 2, :], 1.0).then_inc(s_kone, 1)
            pool.wait_ge(s_vz, 8)
            pool.wait_ge(s_kone, 2)

            with pool.Fori(0, H // 2) as i:
                for g in range(2 * UNITS):
                    if not low_count(g)[0]:
                        take_low(pool, i, g)

            pool.wait_ge(s_zfill, 32)
            pool.wait_ge(s_norm_dve, normed_dve(3))
            pool.wait_ge(s_norm_act, normed_act(3))
            pool.wait_ge(s_idx, 1)
            for t in range(T):
                pool.indirect_dma_start(
                    out=xs0_d[:, :], out_offset=bass.IndirectOffsetOnAxis(ap=idx[:, 0, t:t + 1], axis=0),
                    in_=nat[:, t, :], in_offset=None, bounds_check=SLOTS0 - 1, oob_is_err=False).then_inc(s_scat, 16)
            pool.wait_ge(s_u2, T)
            pool.tensor_tensor(x_res[:, :, :], x_res[:, :, :], u[:, :, :], ALU.add).then_inc(s_x1u, 1)
            pool.wait_ge(s_scat, 16 * T)
            pool.memset(nat[:, :, :], 0.0).then_inc(s_gz, 1)
            pool.wait_ge(s_gz, 1)
            for k in range(2):
                pool.wait_ge(s_ys[k], PRIMED + 32 * (E // 2))
            for t in range(T):
                pool.indirect_dma_start(
                    out=nat[:, t, :], out_offset=None, in_=ys0_d[:, :],
                    in_offset=bass.IndirectOffsetOnAxis(ap=idx[:, 0, t:t + 1], axis=0),
                    bounds_check=SLOTS0 - 1, oob_is_err=False).then_inc(s_gath[t], 16)

            pool.wait_ge(s_norm_dve, normed_dve(5))
            pool.wait_ge(s_norm_act, normed_act(5))
            pool.wait_ge(s_idx, 3)
            for n in range(2):
                for t in range(T):
                    pool.indirect_dma_start(
                        out=xs1_d[:, :], out_offset=bass.IndirectOffsetOnAxis(ap=idx[:, n, t:t + 1], axis=0),
                        in_=nat[:, t, :], in_offset=None, bounds_check=SLOTS1 - 1,
                        oob_is_err=False).then_inc(s_scat1, 16)
            pool.wait_ge(s_scat1, 2 * 16 * T)
            pool.memset(nat[:, :, :], 0.0).then_inc(s_gz, 1)
            pool.memset(u[:, :, :], 0.0).then_inc(s_gz, 1)
            pool.wait_ge(s_gz, 3)
            pool.wait_ge(s_y1o, PRIMED + 16 * TILES1)
            for t in range(T):
                for n, dst in enumerate((nat, u)):
                    pool.indirect_dma_start(
                        out=dst[:, t, :], out_offset=None, in_=ys1_d[:, :],
                        in_offset=bass.IndirectOffsetOnAxis(ap=idx[:, n, t:t + 1], axis=0),
                        bounds_check=SLOTS1 - 1, oob_is_err=False).then_inc(s_gath[t], 16)

        @block.scalar
        def _(act):
            def root(k):
                act.wait_ge(s_var, k)
                act.activation(std[:, :], var[:, :], ACT.Sqrt).then_inc(s_std, 1)

            def turned(r, g, b):
                for n in range(3):
                    lo, hi = 4 * n * P, min(4 * n + 4, T) * P
                    act.wait_ge(s_tr, 6 * r + 2 * n + 1)
                    if g is None:
                        act.activation(nt[:, 0, lo:hi], ps[:, 2 * n, 0:hi - lo], ACT.Identity).then_inc(s_tr_act, 1)
                    else:
                        act.activation(nt[:, 0, lo:hi], ps[:, 2 * n, 0:hi - lo], ACT.Identity,
                                       bias=vecs[:, b:b + 1], scale=vecs[:, g:g + 1]).then_inc(s_tr_act, 1)

            def normed(k, src, dst):
                act.wait_ge(s_rstd, k)
                for t in range(1, T, 2):
                    act.activation(dst[:, t, :], src[:, t, :], ACT.Identity, bias=shift[:, t:t + 1],
                                   scale=rstd[:, t:t + 1]).then_inc(s_norm_act, 1)

            root(1)
            normed(1, x_res, nat)
            root(2)
            root(3)
            normed(2, x_res, nat)
            act.wait_ge(s_wts, WTS)
            turned(0, V_G1, V_B1)
            for n, (hi_d, lo_d, mt, c) in enumerate(qk_chunks):
                v = V_BQ if hi_d is q_hi_d else V_BK
                act.wait_ge(s_qk_ps, n + 1)
                if n >= 2:
                    act.wait_ge(s_qk_lo, n - 1)
                pads = v == V_BK and c == QB - 1
                real = N - c * NC4 if pads else NC4
                last = act.activation(proj[n % 2][:, 0:real], ps[:, n % 8, 0:real], ACT.Identity,
                                      bias=vecs[:, v + mt:v + mt + 1])
                if pads:
                    last = act.activation(proj[n % 2][:, real:NC4], ps[:, (n - c) % 8, 0:NC4 - real], ACT.Identity,
                                          bias=vecs[:, v + mt:v + mt + 1])
                last.then_inc(s_qk_raw, 1)

            def exps(i, g):
                before = i * (2 * UNITS) + g
                act.wait_ge(s_s2, before + 1)
                who, n = low_count(g - 4) if g >= 4 else (by_dve[UNITS - 4 + g], 0)
                act.wait_ge(s_lo[who], PRIMED + lows_taken(i, who) + n)
                act.wait_ge(s_av, PRIMED + (before - 3 if g > 2 else i * (2 * UNITS)))
                src = ps[:, 2 + 2 * (g % 2):4 + 2 * (g % 2), 0:QC]
                act.activation(expo[g % 4][:, :].rearrange("p (c q) -> p c q", c=2), src, ACT.Exp, scale=SCALE)
                act.activation(expo_hi[g % 4][:, :].rearrange("p (c q) -> p c q", c=2), src, ACT.Exp,
                               scale=SCALE).then_inc(s_exp, 1)

            for t in range(T):
                act.activation(u[:, t, :], x_res[:, t, :], ACT.Identity, bias=shift_u[:, t:t + 1],
                               scale=rstd_u[:, t:t + 1]).then_inc(s_u1, 1)
            with act.Fori(0, H // 2) as i:
                for g in range(2 * UNITS):
                    exps(i, g)

            root(4)
            normed(3, u, nat)
            turned(1, V_G2, V_B2)
            act.wait_ge(s_lg, 2)
            act.activation(probs[:, :, :], lg[:, :, :], ACT.Exp).then_inc(s_pexp, 1)

            def expert0(i, k):
                e = i * 2 + k
                act.wait_ge(s_w0[k], i * 16 + 16)
                for f in range(FT):
                    act.wait_ge(s_h0_ps, e * FT + (f + 1))
                    if f == 0:
                        act.wait_ge(s_y0_ps, PRIMED + e)
                    act.activation(h0[:, f, :], ps[:, 2 + f % 2, 0:CAPP], ACT.Gelu,
                                   bias=w_l0[k][:, B1AT + f:B1AT + f + 1]).then_inc(s_h0, 1)

            with act.Fori(0, E // 2) as i:
                expert0(i, 0)
                expert0(i, 1)

            root(5)
            normed(4, x_res, nat)
            turned(2, None, None)
            for t in range(T):
                act.wait_ge(s_hg_ps, t + 1)
                act.copy(hg[:, t, 0:D], ps[:, t % 8, 0:D])
                act.copy(a12[:, t, :], ps[:, t % 8, D:D + 2]).then_inc(s_hg, 1)
            act.wait_ge(s_cexp, 1)
            act.activation(pq[:, 0, :], cneg[:, :], ACT.Exp, scale=0.8)
            act.activation(pq[:, 1, :], cpos[:, :], ACT.Exp, scale=-0.8)
            act.activation(fg[:, 0, :], agap[:, :], ACT.Exp)
            act.activation(fg[:, 1, :], agap[:, :], ACT.Exp, scale=0.2).then_inc(s_pqfg, 1)
            for n in range(3):
                lo, hi = 4 * n * P, min(4 * n + 4, T) * P
                act.wait_ge(s_pqr, 2 * n + 1)
                act.copy(pq_rows[:, 0, lo:hi], ps[:, 2 * n, 0:hi - lo]).then_inc(s_pq_act, 1)
            act.wait_ge(s_pq_act, 3)

            def positive(j, k):
                act.activation(wgt[k][:, :], pq_rows[:, 0, :], ACT.Identity,
                               scale=fg[:, 0, bass.ds(j, 1)]).then_inc(s_t1, 1)

            act.wait_ge(s_pqfg, 1)
            for j in range(2):
                positive(j, j)
            with act.Fori(0, 3) as i:
                for k in range(3):
                    act.wait_ge(s_g1, PRIMED + i * 3 + k)
                    positive(i * 3 + (2 + k), (2 + k) % 3)
            for n in range(2):
                act.wait_ge(s_elu, n + 1)
                lo, hi = ((0, GA), (GA, T))[n]
                ef = hg_flat[:, lo * D:hi * D] if n else elu_exp[:, :]
                act.activation(ef, ef, ACT.Exp).then_inc(s_eexp, 1)

            root(6)
            normed(5, x_res, nat)
            turned(3, None, None)
            act.wait_ge(s_lg, 4)
            act.activation(probs[:, :, :], lg[:, :, :], ACT.Exp).then_inc(s_pexp, 1)
            act.wait_ge(s_te, 1)
            act.wait_ge(s_w1, 32)

            def gelu1(t):
                e = act.value_load(tile_expert[0:1, bass.ds(t, 1)], min_val=0, max_val=E - 1)
                act.wait_ge(s_h1t_ps, t + 1)
                act.wait_ge(s_y1_ps, PRIMED + t)
                for f in range(FT):
                    last = act.activation(h1[:, f, :], ps[:, 4 + f // 4, (f % 4) * P:(f % 4 + 1) * P],
                                          ACT.Gelu_apprx_tanh, bias=w_l1[:, bass.ds(e, 1), B1AT + f])
                last.then_inc(s_h1, 1)

            with act.Fori(0, TILES1) as t:
                gelu1(t)

        @block.tensor
        def _(pe):
            def turn(r, k):
                for n in range(3):
                    pe.wait_ge(s_norm_dve, normed_dve(k, min(4 * n + 3, T - 1)))
                    pe.wait_ge(s_norm_act, normed_act(k, min(4 * n + 3, T - 1)))
                    for c in range(DT):
                        for t in range(4 * n, min(4 * n + 4, T)):
                            last = pe.transpose(ps[:, 2 * n + c, (t - 4 * n) * P:(t - 4 * n + 1) * P],
                                                nat[:, t, c * P:(c + 1) * P], ident)
                        last.then_inc(s_tr, 1)

            def turned(r):
                pe.wait_ge(s_tr_act, 3 * r + 3)
                pe.wait_ge(s_tr_dve, 3 * r + 3)

            def graph0(j, k, first, last):
                pe.wait_ge(s_hid, j + 1)
                for t in range(T):
                    mm = pe.matmul(ps[:, t // 2, (t % 2) * D:(t % 2 + 1) * D], adj0[k][:, t * P:(t + 1) * P],
                                   nat[:, j, :] if first else nat[:, bass.ds(j, 1), :].rearrange("p a d -> p (a d)"),
                                   start=first and t % 2 == 0, stop=last, skip_group_check=True)
                mm.then_inc(s_g0_row, 1)

            for j in range(2):
                pe.wait_ge(s_adj0[j], 16)
                graph0(j, j, j == 0, False)
            with pe.Fori(0, 3) as i:
                for k in range(3):
                    pe.wait_ge(s_adj0[(2 + k) % 3], i * 16 + (16 if k == 0 else 32))
                    graph0(i * 3 + (2 + k), (2 + k) % 3, False, False)

            pe.wait_ge(s_const, 32)
            turn(0, 2)
            turned(0)
            pe.wait_ge(s_wts, WTS)
            for n, (hi_d, lo_d, mt, c) in enumerate(qk_chunks):
                w = w_attn[:, 0 if hi_d is q_hi_d else 1, :, :]
                if n >= 8:
                    pe.wait_ge(s_qk_raw, 4 * ((n - 8) // 4) + 4)
                for kt in range(DT):
                    mm = pe.matmul(ps[:, n % 8, 0:NC4], w[:, kt, mt * P:(mt + 1) * P],
                                   nt[:, kt, c * NC4:(c + 1) * NC4], start=kt == 0, stop=kt == DT - 1)
                mm.then_inc(s_qk_ps, 1)
            for t in range(T):
                if t < 8:
                    pe.wait_ge(s_qk_raw, 8 + 4 * (t // 4) + 4)
                else:
                    pe.wait_ge(s_v, t - 7)
                for kt in range(DT):
                    mm = pe.matmul(ps[:, t % 8, 0:D], nt[:, kt, t * P:(t + 1) * P], w_attn[:, 2, kt, :],
                                   start=kt == 0, stop=kt == DT - 1)
                mm.then_inc(s_v_ps, 1)

            def max_chunk(h, k, n, free):
                if free:
                    pe.wait_ge(s_mx, h * CHUNKS + (n - 1))
                pe.matmul(ps[:, n % 2, 0:QC], q_st[k][0:3 * DK, (n // QB) * P:(n // QB + 1) * P],
                          k_st[k][0:3 * DK, (n % QB) * QC:(n % QB + 1) * QC],
                          start=True, stop=True).then_inc(s_s1, 1)

            def max_rows(h):
                pe.wait_ge(s_hl, h + 1)
                pe.transpose(ps[0:2 * T, 0, 0:P], m_hl.bitcast(F32)[:, :], ident).then_inc(s_mt, 1)

            def scores(i, g, free=False):
                (k, m) = divmod(g % (2 * UNITS), UNITS)
                half, kt = divmod(m, T)
                if m == 0:
                    pe.wait_ge(s_mload[k], (i + g // (2 * UNITS)) * 16 + 16)
                if not free:
                    pe.wait_ge(s_exp, PRIMED + i * (2 * UNITS) + (g - 1))
                for c in range(2):
                    at = half * HALF + c * QC
                    mm = pe.matmul(ps[:, 2 + 2 * (g % 2) + c, 0:QC], k_st[k][0:3 * DK + 2, kt * P:(kt + 1) * P],
                                   q_st[k][0:3 * DK + 2, at:at + QC], start=True, stop=True)
                mm.then_inc(s_s2, 1)

            def values(k, m, c, e, first, last):
                return pe.matmul(ps[0:3 * DK, 6 + c, 0:QC], v_st[k][:, m % T, :], e[:, c * QC:(c + 1) * QC],
                                 start=first and m % T == 0, stop=last and m % T == T - 1)

            def low_values(i, g):
                k, m = divmod(g, UNITS)
                who, n = low_count(g)
                pe.wait_ge(s_lo[who], PRIMED + lows_taken(i, who) + n)
                for c in range(2):
                    mm = values(k, m, c, expo_lo[g % 4], False, True)
                mm.then_inc(s_av, 1)

            def heads(i, last):
                for g in range(2 * UNITS):
                    k, m = divmod(g, UNITS)
                    h = i * 2 + k
                    more = not (last and k)
                    done = sum(beside.get(j, 0) for j in range(m))
                    chunks = list(range(done, done + beside.get(m, 0))) if more else []
                    if m == 0 and more:
                        pe.wait_ge(s_stack[1 - k], i * 96 + (96 if k == 0 else 192))
                        pe.wait_ge(s_mrow, h + 1)
                    if m == 0:
                        pe.wait_ge(s_v_st[k], i * 32 + 32)

                    def chunk():
                        if chunks:
                            max_chunk(h + 1, 1 - k, chunks.pop(0), True)

                    def ahead():
                        if not (last and g + 2 >= 2 * UNITS):
                            scores(i, g + 2)

                    if more and m == MT_AT:
                        max_rows(h + 1)
                    ahead()
                    chunk()
                    if m % T == 0:
                        chunk()
                        pe.wait_ge(s_cr, PRIMED + h * 2 + m // T)
                    pe.wait_ge(s_exp, PRIMED + h * UNITS + (m + 1))
                    for c in range(2):
                        values(k, m, c, expo_hi[g % 4], True, False)
                    chunk()
                    if m % T >= LAG:
                        low_values(i, g - LAG)
                    chunk()
                    if m % T == T - 1:
                        for back in range(LAG - 1, -1, -1):
                            low_values(i, g - back)

            pe.wait_ge(s_v, T)
            pe.wait_ge(s_kone, 2)
            pe.wait_ge(s_vz, 8)
            pe.wait_ge(s_stack[0], 96)
            for n in range(CHUNKS):
                max_chunk(0, 0, n, n >= 2)
            max_rows(0)
            scores(0, 0, free=True)
            scores(0, 1, free=True)
            with pe.Fori(0, H // 2 - 1) as i:
                heads(i, False)
            heads(H // 2 - 1, True)

            pe.wait_ge(s_ctx, 1)
            for t in range(T):
                if t >= 8:
                    pe.wait_ge(s_u2, t - 7)
                for kt in range(DT):
                    mm = pe.matmul(ps[:, t % 8, 0:D], nt[:, kt, t * P:(t + 1) * P], w_attn[:, 3, kt, :],
                                   start=kt == 0, stop=kt == DT - 1)
                mm.then_inc(s_wo, 1)

            def route(layer):
                for c in range(QB):
                    for kt in range(DT):
                        mm = pe.matmul(ps[0:E, 2 + c, 0:NC4], w_router[:, layer, kt, :],
                                       nt[:, kt, c * NC4:(c + 1) * NC4], start=kt == 0, stop=kt == DT - 1)
                mm.then_inc(s_lgt_ps, 1)
                pe.wait_ge(s_lgt, layer + 1)
                for t in range(T):
                    mm = pe.transpose(ps[:, 6, t * E:(t + 1) * E], lgt[:, t * P:(t + 1) * P], const[0:E, C_ID:C_ID + E])
                mm.then_inc(s_lg_ps, 1)
                pe.wait_ge(s_mask, layer + 1)
                pe.matmul(ps[:, 7, 0:T * E], tri_b[:, :], mask_b[:, :, :].rearrange("p t e -> p (t e)"),
                          start=True, stop=False, skip_group_check=True)
                for t in range(T - 1):
                    mm = pe.matmul(ps[:, 7, (t + 1) * E:T * E].rearrange("p (t e) -> p t e", e=E), ones_b[:, :],
                                   mask_b[:, t:t + 1, :].to_broadcast([P, T - 1 - t, E]),
                                   start=False, stop=t == T - 2, skip_group_check=True)
                if layer:
                    for t in range(T):
                        mm = pe.matmul(ps[:, 0, 0:E], ones_b[:, :], mask_b[:, t, :], start=t == 0, stop=t == T - 1)
                mm.then_inc(s_pos, 1)

            turn(1, 3)
            turned(1)
            route(0)

            def xs_in(k, e, need):
                pe.wait_ge(s_xs0[k], need)
                pe.wait_ge(s_xt, e)
                for c in range(DT):
                    for s in range(CT):
                        w = P if s < CT - 1 else CREM
                        mm = pe.transpose(ps[:, c, s * P:s * P + w], xs0[k][0:w, s, c * P:(c + 1) * P],
                                          const[0:w, C_ID:C_ID + w])
                mm.then_inc(s_xt_ps, 1)

            def expert0(i, k, more):
                e = i * 2 + k
                pe.wait_ge(s_w0[k], i * 16 + 16)
                pe.wait_ge(s_xt, e + 1)
                for f in range(FT):
                    pe.wait_ge(s_h0, PRIMED + e * FT + max(f - 1, 0))
                    for kt in range(DT):
                        mm = pe.matmul(ps[:, 2 + f % 2, 0:CAPP], w_l0[k][:, kt * F + f * P:kt * F + (f + 1) * P],
                                       xs0_t[:, kt, :], start=kt == 0, stop=kt == DT - 1)
                    mm.then_inc(s_h0_ps, 1)
                pe.wait_ge(s_yt, PRIMED + e)
                for c in range(DT):
                    for f in range(FT):
                        if c == 0:
                            pe.wait_ge(s_h0, PRIMED + e * FT + (f + 1))
                        at = DT * F + f * D + c * P
                        mm = pe.matmul(ps[:, 4 + c, 0:CAPP], w_l0[k][:, at:at + P], h0[:, f, :],
                                       start=f == 0, stop=f == FT - 1)
                mm.then_inc(s_y0_ps, 1)
                if more:
                    xs_in(1 - k, e + 1, i * 32 + (32 if k == 0 else 64))
                pe.wait_ge(s_yt, PRIMED + e + 1)
                pe.wait_ge(s_yo, PRIMED + e)
                for s in range(CT):
                    w = P if s < CT - 1 else CREM
                    for c in range(DT):
                        mm = pe.transpose(ps[0:w, 6 + s // 2, (s % 2) * D + c * P:(s % 2) * D + (c + 1) * P],
                                          y0_t[:, c, s * P:s * P + w], ident)
                mm.then_inc(s_yo_ps, 1)

            xs_in(0, 0, 32)
            with pe.Fori(0, E // 2 - 1) as i:
                expert0(i, 0, True)
                expert0(i, 1, True)
            expert0(E // 2 - 1, 0, True)
            expert0(E // 2 - 1, 1, False)

            for c in range(DT):
                for kt in range(DT):
                    mm = pe.matmul(ps[:, 2, 2 * c:2 * c + 2], w_graph_t[:, kt, c * P:(c + 1) * P], attn_lr[:, kt, :],
                                   start=kt == 0, stop=kt == DT - 1)
            mm.then_inc(s_wal, 1)
            turn(2, 4)
            turned(2)
            pe.wait_ge(s_wal_sb, 1)
            for t in range(T):
                if t >= 8:
                    pe.wait_ge(s_hg, t - 7)
                for kt in range(DT):
                    mm = pe.matmul(ps[:, t % 8, 0:D + 2], nt[:, kt, t * P:(t + 1) * P], w_graph[:, kt, :],
                                   start=kt == 0, stop=kt == DT - 1)
                mm.then_inc(s_hg_ps, 1)
            pe.wait_ge(s_am, 1)
            pe.transpose(ps[0:1, 7, 0:P], a_max[:, :], ident).then_inc(s_am_t, 1)
            pe.wait_ge(s_am1, 1)
            pe.matmul(ps[:, 6, 0:1], ones[0:1, :], a_max1[:, :], start=True, stop=True).then_inc(s_am_bc, 1)
            pe.wait_ge(s_diag, 2)
            for n in range(3):
                w = (min(4 * n + 4, T) - 4 * n) * P
                for c in range(2):
                    at = c * T + 4 * n
                    pe.matmul(ps[:, 2 * n + c, 0:w], ones[:, :],
                              diag[:, at:at + w // P, :], start=True, stop=True).then_inc(s_pqr, 1)
            pe.wait_ge(s_hg, T)

            def graph1(j, k, first):
                for t in range(GA):
                    mm = pe.matmul(ps[:, t, 0:D + 2], wgt[k][:, t * P:(t + 1) * P],
                                   hg[:, j, :] if first else hg[:, bass.ds(j, 1), :].rearrange("p a d -> p (a d)"),
                                   start=first, stop=False, skip_group_check=True)
                mm.then_inc(s_g1, 1)

            for j in range(2):
                pe.wait_ge(s_w, j + 1)
                graph1(j, j, j == 0)
            with pe.Fori(0, 3) as i:
                for k in range(3):
                    pe.wait_ge(s_w, i * 3 + (3 + k))
                    graph1(i * 3 + (2 + k), (2 + k) % 3, False)
            pe.wait_ge(s_z, GB)
            for t in range(GB):
                for j in range(T):
                    mm = pe.matmul(ps[:, t, 0:D + 2], wgt_keep[:, j, t * P:(t + 1) * P], hg[:, j, :],
                                   start=j == 0, stop=j == T - 1)
                mm.then_inc(s_g1b, 1)

            turn(3, 5)
            turned(3)
            route(1)
            pe.wait_ge(s_idx, 3)
            for t in range(T):
                mm = pe.transpose(ps[0:E, t // 4, (t % 4) * P:(t % 4 + 1) * P], comb[:, t, :], ident)
            mm.then_inc(s_combt_ps, 1)
            pe.wait_ge(s_combt, 1)
            for t in range(T):
                if t >= 6:
                    pe.wait_ge(s_b2_add, t - 5)
                pe.matmul(ps[:, 2 + t % 6, 0:D], comb_t[:, t * P:(t + 1) * P], b2_l1[:, :],
                          start=True, stop=True).then_inc(s_b2, 1)
            pe.wait_ge(s_b2_add, T)
            pe.wait_ge(s_w1, 32)
            pe.wait_ge(s_te, 1)

            def xs1_in(t):
                pe.wait_ge(s_x1l, t * 16 + 16)
                pe.wait_ge(s_x1t, t)
                for c in range(DT):
                    mm = pe.transpose(ps[:, 0, c * P:(c + 1) * P], x1t[:, c * P:(c + 1) * P], ident)
                mm.then_inc(s_x1_ps, 1)

            def up1(t):
                e = pe.value_load(tile_expert[0:1, bass.ds(t, 1)], min_val=0, max_val=E - 1)
                pe.wait_ge(s_x1t, t + 1)
                pe.wait_ge(s_h1pre, t)
                for b in range(2):
                    for kt in range(DT):
                        at = kt * F + b * 512
                        mm = pe.matmul(ps[:, 2 + b, :], x1t_t[:, kt, :],
                                       w_l1[:, bass.ds(e, 1), at:at + 512].rearrange("p a n -> p (a n)"),
                                       start=kt == 0, stop=kt == DT - 1)
                mm.then_inc(s_h1_ps, 1)

            def h1_turn(t):
                pe.wait_ge(s_h1pre, t + 1)
                pe.wait_ge(s_h1, t)
                for f in range(FT):
                    mm = pe.transpose(ps[:, 4 + f // 4, (f % 4) * P:(f % 4 + 1) * P], h1pre[:, f * P:(f + 1) * P], ident)
                mm.then_inc(s_h1t_ps, 1)

            def down1(t):
                e = pe.value_load(tile_expert[0:1, bass.ds(t, 1)], min_val=0, max_val=E - 1)
                pe.wait_ge(s_h1, t + 1)
                pe.wait_ge(s_y1, PRIMED + t)
                for f in range(FT):
                    at = DT * F + f * D
                    mm = pe.matmul(ps[:, 6, 0:D], h1[:, f, :],
                                   w_l1[:, bass.ds(e, 1), at:at + D].rearrange("p a n -> p (a n)"),
                                   start=f == 0, stop=f == FT - 1)
                mm.then_inc(s_y1_ps, 1)

            xs1_in(0)
            up1(0)
            h1_turn(0)
            xs1_in(1)
            with pe.Fori(0, TILES1 - 2) as t:
                up1(t + 1)
                down1(t)
                h1_turn(t + 1)
                xs1_in(t + 2)
            up1(TILES1 - 1)
            down1(TILES1 - 2)
            h1_turn(TILES1 - 1)
            down1(TILES1 - 1)

        @block.vector
        def _(dve):
            steps = [0]

            def step(ins):
                steps[0] += 1
                ins.then_inc(s_step, 1)
                dve.wait_ge(s_step, steps[0])

            roots = [0]

            def inverse_root(v, out):
                roots[0] += 1
                dve.tensor_scalar(var[:, :], v, EPS, None, ALU.add).then_inc(s_var, 1)
                dve.wait_ge(s_std, roots[0])
                step(dve.reciprocal(out[:, :], std[:, :]))

            def minus_mean(factor, out):
                return dve.scalar_tensor_tensor(out=out[:, :], in0=mv[:, :, 0], scalar=-1.0, in1=factor[:, :],
                                                op0=ALU.mult, op1=ALU.mult)

            def moments():
                for t in range(T):
                    last = dve.bn_aggr(mv[:, t, :], stats[:, t, :])
                step(last)

            def apply(t, src, dst):
                return dve.tensor_scalar(dst[:, t, :], src[:, t, :], mv[:, t, 0:1], rstd[:, t:t + 1],
                                         ALU.subtract, ALU.mult)

            def normed(src, dst, masked=False):
                moments()
                inverse_root(mv[:, :, 1], rstd)
                minus_mean(rstd, shift).then_inc(s_rstd, 1)
                for t in range(0, T, 2):
                    last = apply(t, src, dst)
                    if masked and t == T - 1:
                        step(last)
                        last = dve.tensor_scalar(dst[:, t, :], dst[:, t, :], valid[:, t:t + 1], None, ALU.mult)
                    last.then_inc(s_norm_dve, 1)

            def turned(r, g, b):
                for n in range(3):
                    lo, hi = 4 * n * P, min(4 * n + 4, T) * P
                    dve.wait_ge(s_tr, 6 * r + 2 * n + 2)
                    src = ps[:, 2 * n + 1, 0:hi - lo]
                    if g is None:
                        dve.tensor_copy(nt[:, 1, lo:hi], src).then_inc(s_tr_dve, 1)
                    else:
                        dve.tensor_scalar(nt[:, 1, lo:hi], src, vecs[:, g + 1:g + 2], vecs[:, b + 1:b + 2],
                                          ALU.mult, ALU.add).then_inc(s_tr_dve, 1)

            for n, (lo, hi) in enumerate(X_PARTS):
                dve.wait_ge(s_x[n], 16)
                for t in range(lo, hi):
                    last = dve.bn_stats(stats[:, t, :], x_res[:, t, :])
            step(last)
            normed(x_res, nat)
            dve.wait_ge(s_const, 32)
            for t in range(T):
                dve.wait_ge(s_norm_dve, normed_dve(1, t))
                dve.wait_ge(s_norm_act, normed_act(1, t))
                dve.tensor_tensor(nat[:, t, :], nat[:, t, :], rows[:, 2, :], ALU.mult).then_inc(s_hid, 1)
            dve.tensor_copy(tri_b[:, :], const[:, C_TRI:C_TRI + P])
            dve.wait_ge(s_ones, 1)
            dve.tensor_copy(ones_b[:, :], ones[:, :])
            dve.wait_ge(s_g0_row, T)
            for b in range(6):
                w = min(2, T - 2 * b)
                dve.tensor_tensor(x_res[:, 2 * b:2 * b + w, :], x_res[:, 2 * b:2 * b + w, :],
                                  ps[:, b, 0:w * D].rearrange("p (t d) -> p t d", d=D), ALU.add).then_inc(s_x1, 1)
            for t in range(T):
                dve.wait_ge(s_x1, t // 2 + 1)
                last = dve.bn_stats(stats[:, t, :], x_res[:, t, :])
            step(last)

            moments()
            inverse_root(mv[:, :, 1], rstd_u)
            step(dve.tensor_tensor(rstd[:, :], rstd_u[:, :], rstd_u[:, :], ALU.mult))
            step(dve.tensor_tensor(rstd[:, :], rstd[:, :], mv[:, :, 1], ALU.mult))
            inverse_root(rstd[:, :], shift)
            step(dve.tensor_tensor(rstd[:, :], shift[:, :], rstd_u[:, :], ALU.mult))
            minus_mean(rstd_u, shift_u)
            minus_mean(rstd, shift).then_inc(s_rstd, 1)
            for t in range(0, T, 2):
                apply(t, x_res, nat).then_inc(s_norm_dve, 1)
            dve.wait_ge(s_wts, WTS)
            turned(0, V_G1, V_B1)
            for n in range(len(qk_chunks)):
                dve.wait_ge(s_qk_raw, n + 1)
                if n >= 2:
                    dve.wait_ge(s_qk_out[n % 2], 32 * (n // 2))
                dve.tensor_copy(proj_hi[n % 2][:, :], proj[n % 2][:, :]).then_inc(s_qk_hi, 1)
                dve.wait_ge(s_qk_hi, n + 1)
                dve.tensor_tensor(proj_lo[n % 2][:, :], proj[n % 2][:, :], proj_hi[n % 2].bitcast(F32)[:, :],
                                  ALU.subtract).then_inc(s_qk_lo, 1)
            dve.wait_ge(s_vz, 2)
            for t in range(T):
                w = P if t < T - 1 else LAST
                dve.wait_ge(s_v_ps, t + 1)
                dve.tensor_tensor(v_tmp[t % 2][0:w, :], ps[0:w, t % 8, 0:D], rows[0:w, 0, :], ALU.add).then_inc(s_vt, 1)
                dve.wait_ge(s_vt, t + 1)
                dve.tensor_copy(v_hi[0:w, t, :], v_tmp[t % 2][0:w, :]).then_inc(s_vhi, 1)
                dve.wait_ge(s_vhi, t + 1)
                dve.tensor_tensor(v_lo[0:w, t, :], v_tmp[t % 2][0:w, :], v_hi.bitcast(F32)[0:w, t, :],
                                  ALU.subtract).then_inc(s_v, 1)

            def chunk_max(h, n):
                dve.wait_ge(s_s1, h * CHUNKS + (n + 1))
                dve.tensor_reduce(mx4[:, n // QB, n % QB:n % QB + 1], ps[:, n % 2, 0:QC], AX_X, ALU.max).then_inc(s_mx, 1)

            def neg_max(h):
                dve.wait_ge(s_mx, (h + 1) * CHUNKS)
                dve.tensor_reduce(negm[:, :], mx4[:, :, :], AX_X, ALU.max).then_inc(s_mq, 1)
                dve.wait_ge(s_mq, h * 3 + 1)
                dve.tensor_scalar(negm[:, :], negm[:, :], -1.0, None, ALU.mult).then_inc(s_mq, 1)
                dve.wait_ge(s_mt, h)
                dve.wait_ge(s_mq, h * 3 + 2)
                dve.tensor_copy(m_hl[:, 0:T], negm[:, :]).then_inc(s_mq, 1)
                dve.wait_ge(s_mq, h * 3 + 3)
                dve.tensor_tensor(m_hl[:, T:2 * T], negm[:, :], m_hl.bitcast(F32)[:, 0:T],
                                  ALU.subtract).then_inc(s_hl, 1)

            def copy_half(h, half):
                dve.wait_ge(s_av, PRIMED + h * UNITS + T * (half + 1))
                dve.wait_ge(s_cout[half], PRIMED + h * 48)
                dve.tensor_copy(ctx_raw[half][:, :].rearrange("p (c q) -> p c q", c=2),
                                ps[0:3 * DK, 6:8, 0:QC]).then_inc(s_cr, 1)

            def head(i, k, more):
                h = i * 2 + k
                n = 0
                for m in range(UNITS):
                    if m == T:
                        copy_half(h, 0)
                    if by_dve[m]:
                        take_low(dve, i, k * UNITS + m)
                    if more:
                        for _ in range(beside.get(m, 0)):
                            chunk_max(h + 1, n)
                            n += 1
                            if n == CHUNKS:
                                neg_max(h + 1)
                    if more and m == MT_AT:
                        dve.wait_ge(s_mt, h + 2)
                        dve.wait_ge(s_mload[k], i * 16 + 16)
                        dve.tensor_copy(m_rows[:, :], ps[0:2 * T, 0, 0:P]).then_inc(s_mrow, 1)
                copy_half(h, 1)

            for n in range(CHUNKS):
                chunk_max(0, n)
            neg_max(0)
            dve.wait_ge(s_mt, 1)
            dve.tensor_copy(m_rows[:, :], ps[0:2 * T, 0, 0:P]).then_inc(s_mrow, 1)
            dve.wait_ge(s_u1, T)
            step(dve.tensor_tensor(u[:, :, :], u[:, :, :], rows[:, 1:2, :].to_broadcast([P, T, D]), ALU.add))
            with dve.Fori(0, H // 2 - 1) as i:
                head(i, 0, True)
                head(i, 1, True)
            head(H // 2 - 1, 0, True)
            head(H // 2 - 1, 1, False)

            dve.wait_ge(s_den, 16)
            dve.reciprocal(den_all[:, :], den_all[:, :]).then_inc(s_inv, 1)
            dve.wait_ge(s_cin, 32)
            step(dve.tensor_tensor(nt[:, :, :], nt[:, :, :], ctx_low[:, :, :], ALU.add))
            dve.wait_ge(s_inv_in, 16 * DT)
            dve.tensor_tensor(nt[:, :, :], nt[:, :, :], den_rows[:, :, :], ALU.mult).then_inc(s_ctx, 1)
            for t in range(T):
                dve.wait_ge(s_wo, t + 1)
                dve.tensor_tensor(u[:, t, :], u[:, t, :], ps[:, t % 8, 0:D], ALU.add).then_inc(s_u2, 1)
                if t >= 1:
                    dve.wait_ge(s_u2, t)
                    dve.bn_stats(stats[:, t - 1, :], u[:, t - 1, :])
            dve.wait_ge(s_u2, T)
            step(dve.bn_stats(stats[:, T - 1, :], u[:, T - 1, :]))
            normed(u, nat)
            turned(1, V_G2, V_B2)

            def over_e(v):
                return v[:, :, None].to_broadcast([P, T, E])

            def choose(layer):
                dve.wait_ge(s_lgt_ps, layer + 1)
                dve.tensor_scalar(lgt[:, :].rearrange("e (c n) -> e c n", c=QB), ps[0:E, 2:6, 0:NC4],
                                  vecs[0:E, V_RB + layer:V_RB + layer + 1], None, ALU.add).then_inc(s_lgt, 1)
                dve.wait_ge(s_lg_ps, layer + 1)
                dve.tensor_copy(lg[:, :, :], ps[:, 6, 0:T * E].rearrange("p (t e) -> p t e", e=E)).then_inc(s_lg, 1)
                dve.wait_ge(s_lg, 2 * layer + 1)
                step(dve.tensor_reduce(top1[:, :], lg[:, :, :], AX_X, ALU.max))
                step(dve.tensor_tensor(lg[:, :, :], lg[:, :, :], over_e(top1), ALU.subtract))
                dve.tensor_scalar(lg[:, :, :], lg[:, :, :], UNDER, None, ALU.max).then_inc(s_lg, 1)
                dve.wait_ge(s_lg, 2 * layer + 2)
                lj = lg[:, :, :, None].to_broadcast([P, T, E, E])
                li = lg[:, :, None, :].to_broadcast([P, T, E, E])
                dve.tensor_tensor(cmp_gt[:, :, :, :], lj, li, ALU.is_gt)
                step(dve.tensor_tensor(cmp_eq[:, :, :, :], lj, li, ALU.is_equal))
                lower = const[:, C_LT:C_LT + E * E].rearrange("p (o n) -> p o n", o=1).to_broadcast([P, T, E * E])
                eq = cmp_eq[:, :, :, :].rearrange("p t j i -> p t (j i)")
                step(dve.tensor_tensor(eq, eq, lower, ALU.mult))
                step(dve.tensor_tensor(cmp_gt[:, :, :, :], cmp_gt[:, :, :, :], cmp_eq[:, :, :, :], ALU.add))
                step(dve.tensor_reduce(mask[:, :, :], cmp_gt[:, :, :, :].rearrange("p t j i -> p t i j"), AX_X, ALU.add))
                step(dve.tensor_scalar(mask[:, :, :], mask[:, :, :], 1.5, None, ALU.is_lt))
                step(dve.tensor_tensor(mask[:, :, :], mask[:, :, :], over_e(valid), ALU.mult))
                dve.tensor_copy(mask_b[:, :, :], mask[:, :, :]).then_inc(s_mask, 1)

            def row_number(dst, n):
                step(dve.tensor_scalar(skip[:, :], dst[:, :], 0.0, FAR, ALU.is_equal, ALU.mult))
                step(dve.tensor_tensor(skip[:, :], skip[:, :], dst[:, :], ALU.add))
                dve.tensor_scalar(idx[:, n, :], skip[:, :], -1.0, None, ALU.add).then_inc(s_idx, 1)

            choose(0)
            dve.wait_ge(s_pos, 1)
            pos = ps[:, 7, 0:T * E].rearrange("p (t e) -> p t e", e=E)
            off = const[:, C_OFF:C_OFF + E].rearrange("p (o e) -> p o e", o=1).to_broadcast([P, T, E])
            step(dve.tensor_scalar(slot[:, :, :], pos, CAP - 0.5, None, ALU.is_lt))
            step(dve.tensor_tensor(mask[:, :, :], mask[:, :, :], slot[:, :, :], ALU.mult))
            step(dve.tensor_tensor(slot[:, :, :], pos, off, ALU.add))
            step(dve.tensor_tensor(slot[:, :, :], slot[:, :, :], mask[:, :, :], ALU.mult))
            step(dve.tensor_reduce(sa[:, :], slot[:, :, :], AX_X, ALU.max))
            row_number(sa, 0)

            def xs_t(e):
                dve.wait_ge(s_xt_ps, e + 1)
                for c in range(DT):
                    last = dve.tensor_scalar(xs0_t[:, c, :], ps[:, c, 0:CAPP], vecs[:, V_G2 + c:V_G2 + c + 1],
                                             vecs[:, V_B2 + c:V_B2 + c + 1], ALU.mult, ALU.add)
                last.then_inc(s_xt, 1)

            def expert0(i, k, more):
                e = i * 2 + k
                dve.wait_ge(s_y0_ps, PRIMED + e + 1)
                dve.wait_ge(s_yo_ps, PRIMED + e)
                for c in range(DT):
                    last = dve.tensor_scalar(y0_t[:, c, :], ps[:, 4 + c, 0:CAPP], w_l0_b2[k][:, c:c + 1], None, ALU.add)
                last.then_inc(s_yt, 1)
                if more:
                    xs_t(e + 1)
                dve.wait_ge(s_yo_ps, PRIMED + e + 1)
                dve.wait_ge(s_ys[k], PRIMED + i * 32)
                dve.tensor_copy(y0[k][:, 0:2, :], ps[:, 6, :].rearrange("p (s d) -> p s d", d=D))
                dve.tensor_copy(y0[k][0:CREM, 2, :], ps[0:CREM, 7, 0:D]).then_inc(s_yo, 1)

            xs_t(0)
            with dve.Fori(0, E // 2 - 1) as i:
                expert0(i, 0, True)
                expert0(i, 1, True)
            expert0(E // 2 - 1, 0, True)
            expert0(E // 2 - 1, 1, False)
            dve.wait_ge(s_wal, 1)
            dve.tensor_copy(w_graph[:, :, D:D + 2], ps[:, 2, 0:2 * DT].rearrange("p (c n) -> p c n", n=2)).then_inc(s_wal_sb, 1)
            dve.wait_ge(s_x1u, 1)
            for t in range(T):
                dve.wait_ge(s_gath[t], 16)
                dve.tensor_tensor(x_res[:, t, :], x_res[:, t, :], nat[:, t, :], ALU.add).then_inc(s_x2, 1)
                if t >= 1:
                    dve.wait_ge(s_x2, t)
                    dve.bn_stats(stats[:, t - 1, :], x_res[:, t - 1, :])
            dve.wait_ge(s_x2, T)
            step(dve.bn_stats(stats[:, T - 1, :], x_res[:, T - 1, :]))

            normed(x_res, nat, masked=True)
            dve.memset(hg[:, :, D:D + 1], 1.0)
            dve.memset(hg[:, :, D + 1:D + 2], 0.0)
            turned(2, None, None)
            dve.wait_ge(s_hg, T)
            step(dve.tensor_scalar(a_all[:, :], valid[:, T - 1:T], 1.0, 1.0e30, ALU.subtract, ALU.mult))
            step(dve.tensor_tensor(a12[:, T - 1, 1:2], a12[:, T - 1, 1:2], a_all[:, :], ALU.add))
            dve.tensor_reduce(a_max[:, :], a12[:, :, 1], AX_X, ALU.max).then_inc(s_am, 1)
            dve.wait_ge(s_am_t, 1)
            dve.tensor_reduce(a_max1[:, :], ps[0:1, 7, 0:P], AX_X, ALU.max).then_inc(s_am1, 1)
            dve.wait_ge(s_am_bc, 1)
            step(dve.tensor_copy(a_all[:, :], ps[:, 6, 0:1]))
            step(dve.tensor_scalar(csum[:, :], a12[:, :, 0], a_all[:, :], None, ALU.add))
            dve.tensor_scalar(cneg[:, :], csum[:, :], 0.0, None, ALU.min)
            dve.tensor_scalar(cpos[:, :], csum[:, :], 0.0, None, ALU.max)
            dve.tensor_scalar(agap[:, :], a12[:, :, 1], a_all[:, :], None, ALU.subtract).then_inc(s_cexp, 1)
            dve.wait_ge(s_pqfg, 1)
            for c in range(2):
                dve.tensor_tensor(diag[:, c * T:(c + 1) * T, :], ident.rearrange("p (o n) -> p o n", o=1).to_broadcast([P, T, P]),
                                  pq[:, c, :, None].to_broadcast([P, T, P]), ALU.mult).then_inc(s_diag, 1)
            for n in range(3):
                lo, hi = 4 * n * P, min(4 * n + 4, T) * P
                dve.wait_ge(s_pqr, 2 * n + 2)
                dve.tensor_copy(pq_rows[:, 1, lo:hi], ps[:, 2 * n + 1, 0:hi - lo]).then_inc(s_pq_dve, 1)
            dve.wait_ge(s_pq_dve, 3)

            def weigh(j, k, loaded):
                dve.wait_ge(s_t1, j + 1)
                dve.scalar_tensor_tensor(out=wgt[k][:, :], in0=pq_rows[:, 1, :], scalar=fg[:, 1, bass.ds(j, 1)],
                                         in1=wgt[k][:, :], op0=ALU.mult, op1=ALU.max).then_inc(s_t2, 1)
                dve.wait_ge(s_t2, j + 1)
                dve.wait_ge(s_adj1[k], loaded)
                dve.tensor_tensor(wgt_keep[:, bass.ds(j, 1), :].rearrange("p a n -> p (a n)"), wgt[k][:, GA * P:NP],
                                  adj1[k][:, GA * P:NP], ALU.mult)
                dve.tensor_tensor(wgt[k][:, 0:GA * P], wgt[k][:, 0:GA * P], adj1[k][:, 0:GA * P],
                                  ALU.mult).then_inc(s_w, 1)

            for j in range(2):
                weigh(j, j, 16)
            with dve.Fori(0, 3) as i:
                for k in range(3):
                    weigh(i * 3 + (2 + k), (2 + k) % 3, i * 16 + (16 if k == 0 else 32))

            def settle(n, banks, tiles):
                (b0, b1), (lo, hi) = banks, tiles
                step(dve.tensor_scalar(den[:, lo:hi], ps[:, b0:b1, D], 1.0e-9, None, ALU.add))
                step(dve.reciprocal(den[:, lo:hi], den[:, lo:hi]))
                for t in range(lo, hi):
                    dve.tensor_scalar(z[:, t, :], ps[:, b0 + t - lo, 0:D], den[:, t:t + 1], None,
                                      ALU.mult).then_inc(s_z, 1)

            def elu(n, lo, hi):
                dve.wait_ge(s_z, hi)
                zf = z[:, lo:hi, :].rearrange("p t d -> p (t d)")
                ef = hg_flat[:, lo * D:hi * D] if n else elu_exp[:, :]
                xf = x_res[:, lo:hi, :].rearrange("p t d -> p (t d)")
                dve.tensor_scalar(ef, zf, 0.0, None, ALU.min).then_inc(s_elu, 1)
                dve.wait_ge(s_eexp, n + 1)
                step(dve.scalar_tensor_tensor(out=zf, in0=zf, scalar=0.0, in1=ef, op0=ALU.max, op1=ALU.add))
                step(dve.scalar_tensor_tensor(out=xf, in0=zf, scalar=-1.0, in1=xf, op0=ALU.add, op1=ALU.add))
                for t in range(lo, hi):
                    last = dve.bn_stats(stats[:, t, :], x_res[:, t, :])
                return last

            dve.wait_ge(s_g1, PRIMED + T)
            settle(0, (0, GA), (0, GA))
            elu(0, 0, GA)
            dve.wait_ge(s_g1b, GB)
            settle(1, (0, GB), (GA, T))
            step(elu(1, GA, T))

            normed(x_res, nat)
            turned(3, None, None)
            choose(1)
            dve.wait_ge(s_pexp, 2)
            step(dve.tensor_reduce(psum_e[:, :], probs[:, :, :], AX_X, ALU.add))
            step(dve.reciprocal(psum_e[:, :], psum_e[:, :]))
            step(dve.tensor_tensor(probs[:, :, :], probs[:, :, :], over_e(psum_e), ALU.mult))
            step(dve.tensor_tensor(comb[:, :, :], probs[:, :, :], mask[:, :, :], ALU.mult))
            dve.wait_ge(s_pos, 2)
            step(dve.tensor_copy(cnt[:, :], ps[:, 0, 0:E]))
            full = cmp_eq[:, :, :, :].rearrange("p t j i -> p (t j i)")[:, 0:E * T].rearrange("p (e k) -> p e k", k=T)
            step(dve.tensor_tensor(full, cnt[:, :, None].to_broadcast([P, E, T]),
                                   const[:, C_K:C_K + T].rearrange("p (o k) -> p o k", o=1).to_broadcast([P, E, T]),
                                   ALU.is_gt))
            step(dve.tensor_reduce(tiles_e[:, :], full, AX_X, ALU.add))
            upto = cmp_eq[:, :, :, :].rearrange("p t j i -> p (t j i)")[:, 0:E * E].rearrange("p (e k) -> p e k", k=E)
            step(dve.tensor_tensor(upto, const[:, C_LE:C_LE + E * E].rearrange("p (e k) -> p e k", k=E),
                                   tiles_e[:, :].rearrange("p (o k) -> p o k", o=1).to_broadcast([P, E, E]), ALU.mult))
            step(dve.tensor_reduce(ends[:, :], upto, AX_X, ALU.add))
            step(dve.tensor_tensor(starts[:, :], ends[:, :], tiles_e[:, :], ALU.subtract))
            step(dve.tensor_scalar(starts[:, :], starts[:, :], float(P), 1.0, ALU.mult, ALU.add))
            step(dve.tensor_tensor(slot[:, :, :], pos, starts[:, :].rearrange("p (o e) -> p o e", o=1).to_broadcast([P, T, E]),
                                   ALU.add))
            step(dve.tensor_tensor(slot[:, :, :], slot[:, :, :], mask[:, :, :], ALU.mult))
            step(dve.tensor_reduce(sa[:, :], slot[:, :, :], AX_X, ALU.max))
            step(dve.tensor_reduce(sb_[:, :], slot[:, :, :], AX_X, ALU.add))
            step(dve.tensor_tensor(sb_[:, :], sb_[:, :], sa[:, :], ALU.subtract))
            row_number(sa, 0)
            dve.wait_ge(s_idx, 2)
            row_number(sb_, 1)
            step(dve.tensor_tensor(mask[:, :, :], slot[:, :, :], over_e(sa), ALU.is_equal))
            step(dve.tensor_tensor(mask[:, :, :], mask[:, :, :], comb[:, :, :], ALU.mult))
            dve.tensor_reduce(ca[:, :], mask[:, :, :], AX_X, ALU.add)
            step(dve.tensor_reduce(cb[:, :], comb[:, :, :], AX_X, ALU.add))
            step(dve.tensor_tensor(cb[:, :], cb[:, :], ca[:, :], ALU.subtract))
            which = cmp_gt[:, :, :, :].rearrange("p t j i -> p (t j i)")[:, 0:E * (TILES1 + 1)].rearrange("p (k e) -> p k e", e=E)
            step(dve.tensor_tensor(which, const[:, C_TILE:C_TILE + TILES1 + 1, None].to_broadcast([P, TILES1 + 1, E]),
                                   ends[:, :].rearrange("p (o e) -> p o e", o=1).to_broadcast([P, TILES1 + 1, E]),
                                   ALU.is_ge))
            step(dve.tensor_reduce(texp[:, :], which, AX_X, ALU.add))
            dve.tensor_scalar(tile_expert[:, :], texp[:, :], float(E - 1), None, ALU.min).then_inc(s_te, 1)
            dve.wait_ge(s_combt_ps, 1)
            for n in range(3):
                lo, hi = 4 * n * P, min(4 * n + 4, T) * P
                last = dve.tensor_copy(comb_t[:, lo:hi], ps[0:E, n, 0:hi - lo])
            last.then_inc(s_combt, 1)
            for t in range(T):
                dve.wait_ge(s_b2, t + 1)
                dve.tensor_tensor(x_res[:, t, :], x_res[:, t, :], ps[:, 2 + t % 6, 0:D], ALU.add).then_inc(s_b2_add, 1)

            def x1_copy(t):
                dve.wait_ge(s_x1_ps, t + 1)
                dve.wait_ge(s_h1_ps, t)
                dve.tensor_copy(x1t_t[:, :, :], ps[:, 0, 0:DT * P].rearrange("p (c n) -> p c n", n=P)).then_inc(s_x1t, 1)

            def h1_copy(t):
                dve.wait_ge(s_h1_ps, t + 1)
                dve.wait_ge(s_h1t_ps, t)
                dve.tensor_copy(h1pre[:, :].rearrange("p (b n) -> p b n", b=2), ps[:, 2:4, :]).then_inc(s_h1pre, 1)

            def y1_copy(t):
                dve.wait_ge(s_y1_ps, PRIMED + t + 1)
                dve.wait_ge(s_y1o, PRIMED + t * 16)
                dve.tensor_copy(y1t[:, :], ps[:, 6, 0:D]).then_inc(s_y1, 1)

            x1_copy(0)
            h1_copy(0)
            x1_copy(1)
            with dve.Fori(0, TILES1 - 2) as t:
                h1_copy(t + 1)
                y1_copy(t)
                x1_copy(t + 2)
            h1_copy(TILES1 - 1)
            y1_copy(TILES1 - 2)
            y1_copy(TILES1 - 1)
            dve.wait_ge(s_b2_add, T)
            for t in range(T):
                dve.wait_ge(s_gath[t], 3 * 16)
                dve.scalar_tensor_tensor(out=x_res[:, t, :], in0=nat[:, t, :], scalar=ca[:, t:t + 1],
                                         in1=x_res[:, t, :], op0=ALU.mult, op1=ALU.add).then_inc(s_first, 1)
                dve.wait_ge(s_first, t + 1)
                dve.scalar_tensor_tensor(out=x_res[:, t, :], in0=u[:, t, :], scalar=cb[:, t:t + 1],
                                         in1=x_res[:, t, :], op0=ALU.mult, op1=ALU.add).then_inc(s_fin, 1)


def _tiles(w):
    return w.reshape(-1, P, w.shape[-1]).transpose(1, 0, 2)


def _columns(v):
    return v.reshape(-1, P).T


def _experts(w1, b1, w2, b2):
    one = [np.concatenate([_tiles(w1[e]).reshape(P, -1), _tiles(w2[e]).reshape(P, -1), _columns(b1[e])]
                          + ([_columns(b2[e])] if b2 is not None else []), axis=1) for e in range(E)]
    return np.stack(one)


def kernel(**inputs):
    import concourse.bacc as _bacc
    from concourse.bass_utils import run_bass_kernel_spmd as _run

    i = {k: np.asarray(v) for k, v in inputs.items()}
    x = np.zeros((NP, D), np.float32)
    x[:N] = i["x"]
    adj_t = np.zeros((NP, NP), np.float32)
    adj_t[:N, :N] = i["adj"].T
    vecs = np.zeros((P, V_END), np.float32)
    for at, name in ((V_G1, "ln1_g"), (V_B1, "ln1_b"), (V_G2, "ln2_g"), (V_B2, "ln2_b"), (V_BQ, "bq"), (V_BK, "bk")):
        vecs[:, at:at + DT] = _columns(i["L0_ffn_" + name])
    vecs[0:E, V_RB] = i["L0_ffn_router_b"]
    vecs[0:E, V_GB] = i["L1_ffn_bg"]
    arrays = {
        "x": x,
        "adj_t": adj_t,
        "const": shape_constants(),
        "rows": np.concatenate([i["L0_ffn_bv"], i["L0_ffn_bo"], i["L0_gnn_W"]]),
        "vecs": vecs,
        "w_attn": np.stack([_tiles(i["L0_ffn_" + n]) for n in ("wq", "wk", "wv", "wo")], axis=1),
        "w_graph": _tiles(i["L1_gnn_W"]),
        "w_graph_t": _tiles(i["L1_gnn_W"].T),
        "attn_lr": _tiles(np.concatenate([i["L1_gnn_attn_l"], i["L1_gnn_attn_r"]], axis=1)),
        "w_router": np.stack([_tiles(i["L0_ffn_router_w"]), _tiles(i["L1_ffn_Wg"])], axis=1),
        "b2_l1": i["L1_ffn_b2"],
        "w_l0": _experts(i["L0_ffn_w1"], i["L0_ffn_b1"], i["L0_ffn_w2"], i["L0_ffn_b2"]),
        "w_l1": _experts(i["L1_ffn_W1"], i["L1_ffn_b1"], i["L1_ffn_W2"], None).transpose(1, 0, 2),
    }
    arrays = {k: np.ascontiguousarray(v) for k, v in arrays.items()}
    nc = _bacc.Bacc("TRN2", target_bir_lowering=False, num_devices=1)
    aps = {k: nc.dram_tensor(k, v.shape, mybir.dt.from_np(v.dtype), kind="ExternalInput").ap() for k, v in arrays.items()}
    out = nc.dram_tensor("out", (N, D), F32, kind="ExternalOutput").ap()
    build_program(nc, aps, out)
    return _run(nc, [arrays], core_ids=[0]).results[0]["out"]
```
